# Optimizing a Trainium2 kernel written in Bass

```python
import numpy as np
import jax
import jax.numpy as jnp

def _softmax(x, axis=-1):
    return jax.nn.softmax(x, axis=axis)

def _gelu(x):
    return jax.nn.gelu(x, approximate=True)

def _silu(x):
    return jax.nn.silu(x)

def _sigmoid(x):
    return jax.nn.sigmoid(x)

def _layernorm(x, axis=-1, eps=1e-05):
    m = jnp.mean(x, axis=axis, keepdims=True)
    v = jnp.var(x, axis=axis, keepdims=True)
    return (x - m) / jnp.sqrt(v + eps)

def _scatter_add(tgt, idx, src, axis=0):
    return tgt.at[idx].add(src)

def _segment_sum(src, seg, n):
    return jax.ops.segment_sum(src, seg, n)
kernel_name = 'mk_gnn_ffn_d1_gnn_r8_de7a4d'

def setup_inputs(seed: int=0):
    np.random.seed(seed)
    _w = jnp.asarray

    def _rec_inputs():
        import jax
        import jax.numpy as jnp
        _gk = jax.random.key(seed)
        x = -8.776e-05 + 1 * jax.random.normal(jax.random.fold_in(_gk, 1), (2500, 256), jnp.float32)
        src = jax.random.randint(jax.random.fold_in(_gk, 2), (40000,), 0, 2500, jnp.int32)
        dst = jnp.minimum((2500 * jax.random.uniform(jax.random.fold_in(_gk, 3), (40000,)) ** 2.0).astype(jnp.int32), 19999)
        _o = jnp.argsort(dst, stable=True)
        src = src[_o]
        dst = dst[_o]
        edge_type_8 = jax.random.randint(jax.random.fold_in(_gk, 12), (40000,), 0, 8, jnp.int32)
        return (x, src, dst, edge_type_8)
    x, src, dst, edge_type_8 = _rec_inputs()

    def _L0_gnn_setup():
        import jax, jax.numpy as jnp
        import numpy as np
        N_NODES = 2500
        N_EDGES = 40000
        D = 256
        R = 8

        def _xavier(key, shape):
            fan_in, fan_out = (shape[-2], shape[-1])
            bound = float(np.sqrt(6.0 / (fan_in + fan_out)))
            return jax.random.uniform(key, shape, jnp.float32, -bound, bound)

        def _rgcn_layer(x, W, self_w, b, src, dst, edge_type, num_nodes):
            xW = jnp.einsum('ni,rio->rno', x, W)
            msg = xW[edge_type, src]
            agg = jax.ops.segment_sum(msg, dst, num_segments=num_nodes)
            return agg + x @ self_w + b
        key = jax.random.key(seed)
        ks = jax.random.split(key, 10)
        x = jax.random.normal(ks[0], (N_NODES, D), jnp.float32)
        edge_index = jax.random.randint(ks[1], (2, N_EDGES), 0, N_NODES)
        edge_type = jax.random.randint(ks[2], (N_EDGES,), 0, R)
        W1 = _xavier(ks[3], (R, D, D))
        self_w1 = _xavier(ks[4], (D, D))
        b1 = jnp.zeros((D,), jnp.float32)
        W2 = _xavier(ks[5], (R, D, D))
        self_w2 = _xavier(ks[6], (D, D))
        b2 = jnp.zeros((D,), jnp.float32)
        return {'x': x, 'W1': W1, 'self_w1': self_w1, 'b1': b1, 'W2': W2, 'self_w2': self_w2, 'b2': b2, 'edge_index': edge_index, 'edge_type': edge_type}
    _L0_gnn_all = _L0_gnn_setup()
    _L0_gnn_in = {k: v for k, v in _L0_gnn_all.items() if k in ('W1', 'self_w1', 'b1', 'W2', 'self_w2', 'b2')}
    del _L0_gnn_all

    def _L0_ffn_setup():
        import jax, jax.numpy as jnp
        import numpy as np
        DIM = 256
        H = 8
        D = 64
        G = 64
        INNER = H * D
        SCALE = D ** (-0.5)
        key = jax.random.key(seed)
        ks = jax.random.split(key, 12)
        B, N = (4, 2048)
        x = jax.random.normal(ks[0], (B, N, DIM), dtype=jnp.float32)
        s = lambda fan_in: 1.0 / np.sqrt(fan_in)
        W_fx = jax.random.normal(ks[1], (DIM, INNER), dtype=jnp.float32) * s(DIM)
        b_fx = jnp.zeros((INNER,), dtype=jnp.float32)
        W_x = jax.random.normal(ks[2], (DIM, INNER), dtype=jnp.float32) * s(DIM)
        b_x = jnp.zeros((INNER,), dtype=jnp.float32)
        A = jax.random.normal(ks[3], (G, D), dtype=jnp.float32)
        Q, _ = jnp.linalg.qr(A.T)
        W_slice = Q[:, :G].astype(jnp.float32)
        b_slice = jnp.zeros((G,), dtype=jnp.float32)
        W_q = jax.random.normal(ks[4], (D, D), dtype=jnp.float32) * s(D)
        W_k = jax.random.normal(ks[5], (D, D), dtype=jnp.float32) * s(D)
        W_v = jax.random.normal(ks[6], (D, D), dtype=jnp.float32) * s(D)
        W_out = jax.random.normal(ks[7], (INNER, DIM), dtype=jnp.float32) * s(INNER)
        b_out = jnp.zeros((DIM,), dtype=jnp.float32)
        temperature = jnp.ones((1, H, 1, 1), dtype=jnp.float32) * 0.5
        return {'x': x, 'W_fx': W_fx, 'b_fx': b_fx, 'W_x': W_x, 'b_x': b_x, 'W_slice': W_slice, 'b_slice': b_slice, 'W_q': W_q, 'W_k': W_k, 'W_v': W_v, 'W_out': W_out, 'b_out': b_out, 'temperature': temperature}
    _L0_ffn_all = _L0_ffn_setup()
    _L0_ffn_in = {k: v for k, v in _L0_ffn_all.items() if k in ('W_fx', 'b_fx', 'W_x', 'b_x', 'W_slice', 'b_slice', 'W_q', 'W_k', 'W_v', 'W_out', 'b_out', 'temperature')}
    del _L0_ffn_all
    return {'x': x, 'src': src, 'dst': dst, 'edge_type_8': edge_type_8, 'L0_gnn_W1': _L0_gnn_in['W1'], 'L0_gnn_self_w1': _L0_gnn_in['self_w1'], 'L0_gnn_b1': _L0_gnn_in['b1'], 'L0_gnn_W2': _L0_gnn_in['W2'], 'L0_gnn_self_w2': _L0_gnn_in['self_w2'], 'L0_gnn_b2': _L0_gnn_in['b2'], 'L0_ffn_W_fx': _L0_ffn_in['W_fx'], 'L0_ffn_b_fx': _L0_ffn_in['b_fx'], 'L0_ffn_W_x': _L0_ffn_in['W_x'], 'L0_ffn_b_x': _L0_ffn_in['b_x'], 'L0_ffn_W_slice': _L0_ffn_in['W_slice'], 'L0_ffn_b_slice': _L0_ffn_in['b_slice'], 'L0_ffn_W_q': _L0_ffn_in['W_q'], 'L0_ffn_W_k': _L0_ffn_in['W_k'], 'L0_ffn_W_v': _L0_ffn_in['W_v'], 'L0_ffn_W_out': _L0_ffn_in['W_out'], 'L0_ffn_b_out': _L0_ffn_in['b_out'], 'L0_ffn_temperature': _L0_ffn_in['temperature']}

def reference(x, src, dst, edge_type_8, L0_gnn_W1, L0_gnn_self_w1, L0_gnn_b1, L0_gnn_W2, L0_gnn_self_w2, L0_gnn_b2, L0_ffn_W_fx, L0_ffn_b_fx, L0_ffn_W_x, L0_ffn_b_x, L0_ffn_W_slice, L0_ffn_b_slice, L0_ffn_W_q, L0_ffn_W_k, L0_ffn_W_v, L0_ffn_W_out, L0_ffn_b_out, L0_ffn_temperature):
    import jax
    import jax.numpy as jnp

    def _L0_gnn_ref(x, W1, self_w1, b1, W2, self_w2, b2, edge_index, edge_type):
        import jax, jax.numpy as jnp
        import numpy as np
        N_NODES = 2500
        N_EDGES = 40000
        D = 256
        R = 8

        def _xavier(key, shape):
            fan_in, fan_out = (shape[-2], shape[-1])
            bound = float(np.sqrt(6.0 / (fan_in + fan_out)))
            return jax.random.uniform(key, shape, jnp.float32, -bound, bound)

        def _rgcn_layer(x, W, self_w, b, src, dst, edge_type, num_nodes):
            xW = jnp.einsum('ni,rio->rno', x, W)
            msg = xW[edge_type, src]
            agg = jax.ops.segment_sum(msg, dst, num_segments=num_nodes)
            return agg + x @ self_w + b
        src, dst = (edge_index[0], edge_index[1])
        h = _rgcn_layer(x, W1, self_w1, b1, src, dst, edge_type, N_NODES)
        h = jax.nn.relu(h)
        out = _rgcn_layer(h, W2, self_w2, b2, src, dst, edge_type, N_NODES)
        return out

    def _L0_ffn_ref(x, W_fx, b_fx, W_x, b_x, W_slice, b_slice, W_q, W_k, W_v, W_out, b_out, temperature):
        import jax, jax.numpy as jnp
        import numpy as np
        DIM = 256
        H = 8
        D = 64
        G = 64
        INNER = H * D
        SCALE = D ** (-0.5)
        B, N, _ = x.shape
        fx_mid = (x @ W_fx + b_fx).reshape(B, N, H, D).transpose(0, 2, 1, 3)
        x_mid = (x @ W_x + b_x).reshape(B, N, H, D).transpose(0, 2, 1, 3)
        temp = jnp.clip(temperature, 0.1, 5.0)
        slice_weights = jax.nn.softmax((x_mid @ W_slice + b_slice) / temp, axis=-1)
        slice_norm = slice_weights.sum(axis=2)
        slice_token = jnp.einsum('bhnc,bhng->bhgc', fx_mid, slice_weights)
        slice_token = slice_token / (slice_norm[..., None] + 1e-05)
        q = slice_token @ W_q
        k = slice_token @ W_k
        v = slice_token @ W_v
        attn = jax.nn.softmax(jnp.einsum('bhgc,bhkc->bhgk', q, k) * SCALE, axis=-1)
        out_slice = jnp.einsum('bhgk,bhkc->bhgc', attn, v)
        out_x = jnp.einsum('bhgc,bhng->bhnc', out_slice, slice_weights)
        out_x = out_x.transpose(0, 2, 1, 3).reshape(B, N, INNER)
        return out_x @ W_out + b_out
    edge_index = jnp.stack([src, dst])
    x = x + _L0_gnn_ref(_layernorm(x, axis=-1), L0_gnn_W1, L0_gnn_self_w1, L0_gnn_b1, L0_gnn_W2, L0_gnn_self_w2, L0_gnn_b2, edge_index, edge_type_8)
    x = x + _L0_ffn_ref(_layernorm(x, axis=-1)[None], L0_ffn_W_fx, L0_ffn_b_fx, L0_ffn_W_x, L0_ffn_b_x, L0_ffn_W_slice, L0_ffn_b_slice, L0_ffn_W_q, L0_ffn_W_k, L0_ffn_W_v, L0_ffn_W_out, L0_ffn_b_out, L0_ffn_temperature)[0]
    return x

_drawn_inputs = setup_inputs


def setup_inputs(seed=0):
    import zlib

    import numpy as np

    out = dict(_drawn_inputs(seed))
    spreads = {'L0_gnn_b1': (0.0, 0.1),
     'L0_gnn_b2': (0.0, 0.8),
     'L0_ffn_b_fx': (0.0, 0.8),
     'L0_ffn_b_x': (0.0, 0.8),
     'L0_ffn_b_slice': (0.0, 0.8),
     'L0_ffn_b_out': (0.0, 0.8),
     'L0_ffn_temperature': (0.5, 0.6)}
    factors = {'L0_ffn_W_x': 8.0, 'L0_ffn_W_slice': 8.0, 'L0_ffn_W_q': 8.0, 'L0_ffn_W_k': 8.0}
    for name, (base, spread) in spreads.items():
        noise = np.random.default_rng([zlib.crc32(name.encode()), seed]).standard_normal(out[name].shape)
        drawn = base * np.exp(spread * noise) if base else spread * noise
        out[name] = jnp.asarray(drawn.astype(out[name].dtype))
    for name, factor in factors.items():
        out[name] = (out[name] * factor).astype(out[name].dtype)
    return out
```

```python
import concourse.bass as bass
from concourse import mybir
from contextlib import ExitStack
import numpy as np

f32 = mybir.dt.float32
bf16 = mybir.dt.bfloat16
i32 = mybir.dt.int32
u32 = mybir.dt.uint32
ALU = mybir.AluOpType
ACT = mybir.ActivationFunctionType
AX = mybir.AxisListType

P = 128
N, E, D, R = 2500, 40000, 256, 8
K2 = D // P
NT = -(-N // P)
TAIL = N - (NT - 1) * P
ET = -(-E // P)
EC = -(-ET // P)
RING = 16
HALF = RING // 2
STEPS = -(-(ET + NT - 1) // RING) * RING
GROUPS = STEPS // RING
ROW = 3 * D
CH = 4
CW = R * D // CH
H, C, G = 8, 64, 64
HP = H // 2
HG = H * G
EPS_LN = 1e-5
EPS_SLICE = 1e-5
SCALE = float(C) ** -0.5
NO_NODE = 4096


class Chain:

    def __init__(self, eng, sem, it=0, per_turn=0):
        self.eng, self.sem, self.base, self.n = eng, sem, it * per_turn, 0

    def done(self, ins):
        self.n += 1
        ins.then_inc(self.sem, 1)
        self.eng.wait_ge(self.sem, self.base + self.n)


def rgcn_slice_attention(nc, x, src, dst, rel, W1, self_w1, b1, W2, self_w2, b2, W_fx, b_fx, W_x, b_x,
                         W_slice, b_slice, W_q, W_k, W_v, W_out, b_out, temperature, out):
    msg1 = nc.dram_tensor("msg1", (NT * P * R, ROW), bf16, kind="Internal").ap()
    msg2 = nc.dram_tensor("msg2", (NT * P * R, ROW), bf16, kind="Internal").ap()
    msg_tiles = [m.rearrange("(t p r) d -> t p (r d)", p=P, r=R) for m in (msg1, msg2)]

    with ExitStack() as ctx:
        ctx.enter_context(nc.allow_non_contiguous_dma(reason="a few small columns of biases and indices"))
        sb = lambda name, shape, dt=f32: ctx.enter_context(nc.sbuf_tensor(name, shape, dt))
        sem = lambda name: ctx.enter_context(nc.semaphore(name))

        onehot = sb("onehot", [P, STEPS, P], bf16)
        ring = sb("ring", [P, RING, ROW], bf16)
        base = sb("base", [P, NT, D])
        area = sb("area", [P, HP * NT * P])
        wrel = area[:, 0:K2 * R * D].rearrange("p (k m) -> p k m", k=K2)
        o = K2 * R * D
        parts = area[:, o:o + CH * 2 * ROW // 2].bitcast(bf16).rearrange("p (c r h d) -> p c r h d", c=CH, r=2, h=3)
        o += CH * 2 * ROW // 2
        resid = area[:, o:o + 2 * CW].rearrange("p (b m) -> p b m", b=2)
        swT = area[:, :].rearrange("p (a n) -> p a n", a=HP)
        idx = sb("idx", [P, STEPS], i32)
        idx_now = sb("idx_now", [P, RING], u32)
        seg = sb("seg", [P, STEPS])
        wself = sb("wself", [P, K2, D])
        wfx = sb("wfx", [P, K2, HG])
        wlog = sb("wlog", [P, K2, HG])
        wout = sb("wout", [P, HP, D])
        b1_bo = sb("b1_bo", [P, D])
        b2_all = sb("b2_all", [P, D])
        blog = sb("blog", [P, HG])
        xin = sb("xin", [P, 2, D])
        xn = sb("xn", [P, 2, D])
        xT = sb("xT", [P, 2, K2, P])
        logit = sb("logit", [P, HG])
        sw = sb("sw", [P, HG])
        swsum = sb("swsum", [P, HG])
        ident = sb("ident", [P, P])
        ones = sb("ones", [P, P])
        zeros = sb("zeros", [P, D], bf16)
        bd = {n: sb(f"bd_{n}", [P, P]) for n in ("s", "q", "k", "v")}
        bfx_col = sb("bfx_col", [P, HP])
        bx_col = sb("bx_col", [P, HP])
        ends = sb("ends", [1, P], i32)
        eps = sb("eps", [P, 1])
        mask = sb("mask", [P, NT])
        stats = sb("stats", [P, 6])
        mv = sb("mv", [P, 2, 2])
        std = sb("std", [P, 2, 1])
        rstd = sb("rstd", [P, 2, 1])
        hmax = sb("hmax", [P, H])
        hsum = sb("hsum", [P, H])

        ringf = ring[:, :, :].rearrange("p s d -> p (s d)").bitcast(f32)
        ringi = ring[:, :, :].rearrange("p s d -> p (s d)").bitcast(i32)
        at = [0]

        def cut(view, *dims):
            n = int(np.prod(dims))
            got = view[:, at[0]:at[0] + n]
            at[0] += n
            return got.rearrange("p (a b) -> p a b", a=dims[0]) if len(dims) == 2 else got

        src_t, dst_t, rel_t = (cut(ringi, EC, P) for _ in range(3))
        nxt_t, lo_i, hi_i = (cut(ringi, EC) for _ in range(3))
        tile_no = cut(ringf, EC)
        start_lo, start_hi = cut(ringf, EC), cut(ringf, EC)
        row_f, dst_f = cut(ringf, EC, P), cut(ringf, EC, P)
        ge_lo, ge_hi = cut(ringf, EC, STEPS), cut(ringf, EC, STEPS)
        step_no = cut(ringf, STEPS)
        nt_of = cut(ringf, STEPS)
        endc = cut(ringf, 1)
        part_no = cut(ringf, 1)
        assert at[0] <= RING * ROW // 2
        ohf = onehot[:, :, :].rearrange("p s n -> p (s n)").bitcast(f32)
        wx = ohf[:, 0:K2 * HG].rearrange("p (k m) -> p k m", k=K2)
        wxT = ohf[:, 1024:1024 + D]
        bx_all = ohf[:, 1536:1536 + P * HP].rearrange("p (a n) -> p a n", a=HP)
        temp_all = ohf[:, 2048:2048 + H]
        itemp = ohf[:, 2064:2064 + H]
        bsl = ohf[:, 2080:2080 + G]
        le = ohf[:, 2304:2304 + STEPS]
        node_no = sb("node_no", [P, P], bf16)
        at[0] = 0
        ttn = cut(ringf, K2, HG)
        rnorm = cut(ringf, HG)
        cnorm = cut(ringf, HG)
        tokC = cut(ringf, HP, G)
        qkvT = [cut(ringf, HP, G) for _ in range(3)]
        att = cut(ringf, HP, G)
        attT = cut(ringf, HP, P)
        vo = cut(ringf, H, D)
        amax, asum = cut(ringf, HP), cut(ringf, HP)
        assert at[0] <= RING * ROW // 2
        mix = onehot[:, 0:16, :].rearrange("p s n -> p (s n)").bitcast(f32).rearrange("p (a d) -> p a d", a=HP)
        swTile = onehot[:, 16:32, :].rearrange("p s n -> p (s n)").bitcast(f32).rearrange("p (b a n) -> p b a n", b=2, a=HP)
        res = onehot[:, 32:48, :].rearrange("p s n -> p (s n)").bitcast(f32)[:, 0:2 * D].rearrange("p (b d) -> p b d", b=2)

        bank = {n: ctx.enter_context(nc.psum_tensor(n, [P, 512], f32))
                for n in ("agg", "tr", "self", "c0", "c1", "t0", "t1", "misc")}
        agg, chunk = bank["agg"][:, 0:D], [bank["c0"], bank["c1"]]

        xin_full = [sem("xin_full0"), sem("xin_full1")]
        part_sent = [sem(f"part_sent{c}") for c in range(CH)]
        slot_full = [sem(f"slot_full{i}") for i in range(RING)]
        res_sent = [sem("res_sent0"), sem("res_sent1")]
        names = """pads_set consts_set ld_edges ld_small ld_w1 ld_w2 ld_bo dve_prep edges_ready step_mm endc_ready
        ends_mm ends_ready bx_ready wxT_mm wxT_saved wlog_mm wlog_saved onehot_ready
        var_ready std_ready xn_ready tr_done xT_ready self_free self_mm chunk_mm hi_ready res_ready mid_ready lo_ready
        idx_copied rows_ready ring_free agg_done agg_free base_ready
        logit_mm logit_ready exp_ready sw_ready swT_done swT_saved
        norm1_steps norm2_steps base_steps slice_steps swsum_steps tail_steps
        norm_mm ttn_ready tok_mm tok_ready qkv_mm qkv_saved score_mm score_ready score_exp att_ready attT_mm attT_saved
        vo_mm vo_saved mix_mm mix_saved tile_copied out_mm out_added out_ready""".split()
        sems = {name: sem(name) for name in names}
        (pads_set, consts_set, ld_edges, ld_small, ld_w1, ld_w2, ld_bo, dve_prep, edges_ready, step_mm, endc_ready,
         ends_mm, ends_ready, bx_ready, wxT_mm, wxT_saved, wlog_mm, wlog_saved, onehot_ready,
         var_ready, std_ready, xn_ready, tr_done, xT_ready, self_free, self_mm, chunk_mm, hi_ready, res_ready, mid_ready, lo_ready,
         idx_copied, rows_ready, ring_free, agg_done, agg_free, base_ready,
         logit_mm, logit_ready, exp_ready, sw_ready, swT_done, swT_saved,
         norm1_steps, norm2_steps, base_steps, slice_steps, swsum_steps, tail_steps,
         norm_mm, ttn_ready, tok_mm, tok_ready, qkv_mm, qkv_saved, score_mm, score_ready, score_exp, att_ready, attT_mm, attT_saved,
         vo_mm, vo_saved, mix_mm, mix_saved, tile_copied, out_mm, out_added, out_ready) = (sems[name] for name in names)

        VO_BANKS, MIX_BANKS = ("agg", "tr", "self", "c1"), ("t0", "t1")

        past = {e.engine: sem(f"past_{n}") for n, e in (("pool", nc.gpsimd), ("act", nc.scalar), ("dve", nc.vector))}

        def alone(eng):
            eng.sem_inc(past[eng.engine], 1)

        def tile_at(view, j):
            return view[:, bass.ds(j, 1), :].rearrange("p a n -> p (a n)")

        def heads(view):
            return view.rearrange("p (h g) -> p h g", g=G)

        block = ctx.enter_context(nc.Block())

        EDGE_LOADS, SMALL_LOADS = 4 * 3 + EC, 17

        @block.sync
        def _(sp):
            sp.wait_ge(pads_set, 1)
            whole = (E // P) * P
            for arr, t in ((dst, dst_t), (src, src_t), (rel, rel_t)):
                for c in range(EC):
                    lo, hi = c * P * P, min((c + 1) * P * P, whole)
                    sp.dma_start(t[0:(hi - lo) // P, c, :], arr[lo:hi].rearrange("(t e) -> t e", e=P)).then_inc(ld_edges, 16)
                r0 = whole // P - (EC - 1) * P
                sp.dma_start(t[r0:r0 + 1, EC - 1, 0:E - whole], arr[whole:E].rearrange("(t e) -> t e", t=1)).then_inc(ld_edges, 16)
            firsts = dst[P:E:P].rearrange("(t e) -> t e", e=1)
            for c in range(EC):
                m = min(P, ET - 1 - c * P)
                sp.dma_start(nxt_t[0:m, c:c + 1], firsts[c * P:c * P + m, :]).then_inc(ld_edges, 16)
            for par in range(2):
                sp.dma_start(xin[:, par, :], x[par * P:(par + 1) * P, :]).then_inc(xin_full[par], 16)
            for k in range(K2):
                sp.dma_start(wrel[:, k, :].rearrange("p (r m) -> p r m", r=R), W1[:, k * P:(k + 1) * P, :].rearrange("r p m -> p r m")).then_inc(ld_w1, 16)
            sp.dma_start(wself[:, :, :], self_w1.rearrange("(k p) m -> p k m", p=P)).then_inc(ld_w1, 16)

            def send_table(jj, full):
                for par in range(2):
                    j = jj * 2 + par
                    for c in range(CH):
                        sp.wait_ge(lo_ready, j * CH + c + 1)
                        sp.dma_start(msg_tiles[0][bass.ds(j, 1), :, c * 2 * ROW:(c + 1) * 2 * ROW].rearrange("a p d -> (a p) d"),
                                     parts[:, c, :, :, :].rearrange("p r h d -> p (r h d)")).then_inc(part_sent[c], 16)
                    if full:
                        sp.wait_ge(xn_ready, j + 1)
                    if par < full:
                        sp.dma_start(xin[:, par, :], x[bass.ds((j + 2) * P, P), :]).then_inc(xin_full[par], 16)
                    elif full:
                        sp.dma_start(xin[0:TAIL, par, :], x[N - TAIL:N, :]).then_inc(xin_full[par], 16)

            with sp.Fori(0, NT // 2 - 2) as jj:
                send_table(jj, 2)
            send_table(NT // 2 - 2, 1)
            send_table(NT // 2 - 1, 0)
            sp.wait_ge(chunk_mm, NT * CH)
            for k in range(K2):
                sp.dma_start(wrel[:, k, :].rearrange("p (r m) -> p r m", r=R), W2[:, k * P:(k + 1) * P, :].rearrange("r p m -> p r m")).then_inc(ld_w2, 16)
            sp.dma_start(wself[:, :, :], self_w2.rearrange("(k p) m -> p k m", p=P)).then_inc(ld_w2, 16)
            with sp.Fori(0, 2 * GROUPS) as g:
                for i in range(RING):
                    sp.wait_ge(slot_full[i], (g + 1) * 16)
                    sp.sem_inc(rows_ready, 1)
            with sp.Fori(0, NT // 2 - 1) as jj:
                for par in range(2):
                    sp.wait_ge(out_ready, jj * 2 + par + 1)
                    sp.dma_start(out[bass.ds((jj * 2 + par) * P, P), :], res[:, par, :]).then_inc(res_sent[par], 16)
            sp.wait_ge(out_ready, NT - 1)
            sp.dma_start(out[(NT - 2) * P:(NT - 1) * P, :], res[:, 0, :]).then_inc(res_sent[0], 16)
            sp.wait_ge(out_ready, NT)
            sp.dma_start(out[N - TAIL:N, :], res[0:TAIL, 1, :]).then_inc(res_sent[1], 16)
            for par in range(2):
                sp.wait_ge(res_sent[par], 16 * (NT // 2))

        @block.gpsimd
        def _(pool):
            nc.gpsimd.memset(dst_t, NO_NODE)
            nc.gpsimd.memset(src_t, 0)
            nc.gpsimd.memset(rel_t, 0)
            nc.gpsimd.memset(nxt_t, NO_NODE).then_inc(pads_set, 1)
            nc.gpsimd.memset(ones[:, :], 1.0)
            nc.gpsimd.memset(zeros[:, :], 0.0)
            nc.gpsimd.memset(swsum[:, :], 0.0)
            nc.gpsimd.memset(eps[:, :], EPS_LN)
            nc.gpsimd.memset(mask[:, :], 1.0)
            for m in bd.values():
                nc.gpsimd.memset(m[:, :], 0.0)
            nc.gpsimd.iota(tile_no, [[P, EC]], base=0, channel_multiplier=1, allow_small_or_imprecise_dtypes=True)
            nc.gpsimd.iota(step_no, [[1, STEPS]], base=0, channel_multiplier=0, allow_small_or_imprecise_dtypes=True)
            nc.gpsimd.iota(part_no, [[0, 1]], base=0, channel_multiplier=1, allow_small_or_imprecise_dtypes=True)
            nc.gpsimd.iota(node_no[:, :], [[1, P]], base=0, channel_multiplier=0, allow_small_or_imprecise_dtypes=True)
            nc.gpsimd.memset(ident[:, :], 0.0).then_inc(pads_set, 1)
            pool.wait_ge(pads_set, 2)
            nc.gpsimd.affine_select(out=ident[:, :], in_=ident[:, :], compare_op=ALU.not_equal, fill=1.0, base=0,
                                    pattern=[[-1, P]], channel_multiplier=1)
            last = mask[:, NT - 1:NT]
            nc.gpsimd.affine_select(out=last, in_=last, compare_op=ALU.is_gt, fill=0.0, base=TAIL,
                                    pattern=[[0, 1]], channel_multiplier=-1).then_inc(consts_set, 1)
            def gather(layer):
                with pool.Fori(0, GROUPS) as g:
                    for h in range(2):
                        pool.wait_ge(ring_free, (g + layer * GROUPS) * RING + (h + 1) * HALF)
                        nc.gpsimd.tensor_copy(idx_now[:, h * HALF:(h + 1) * HALF],
                                              idx[:, bass.ds(g * RING + h * HALF, HALF)]).then_inc(idx_copied, 1)
                        pool.wait_ge(idx_copied, (g + layer * GROUPS) * 2 + h + 1)
                        alone(pool)
                        for i in range(h * HALF, (h + 1) * HALF):
                            nc.gpsimd.indirect_dma_start(
                                ring[:, i, :], None, (msg1, msg2)[layer],
                                bass.IndirectOffsetOnAxis(ap=idx_now[:, i:i + 1], axis=0)).then_inc(slot_full[i], 16)

            for layer in range(2):
                for c in range(CH):
                    pool.wait_ge(part_sent[c], 16 * NT * (layer + 1))
                gather(layer)

        @block.scalar
        def _(act):
            n = 0
            act.wait_ge(consts_set, 1)
            for name, w in (("s", W_slice), ("q", W_q), ("k", W_k), ("v", W_v)):
                for h2 in range(2):
                    act.dma_start(bd[name][h2 * C:(h2 + 1) * C, h2 * C:(h2 + 1) * C], w).then_inc(ld_small, 16)
                    n += 1
            for t, a in ((b1_bo, b1), (b2_all, b2)):
                act.dma_start(t[:, :], a.rearrange("(a n) -> a n", a=1).to_broadcast([P, D])).then_inc(ld_small, 16)
                n += 1
            act.dma_start(bsl, b_slice.rearrange("(a n) -> a n", a=1).to_broadcast([P, G])).then_inc(ld_small, 16)
            act.dma_start(temp_all, temperature.rearrange("a h b c -> a (h b c)").to_broadcast([P, H])).then_inc(ld_small, 16)
            act.dma_start(bfx_col[:, :], b_fx.rearrange("(a p) -> p a", p=P)).then_inc(ld_small, 16)
            act.dma_start(bx_col[:, :], b_x.rearrange("(a p) -> p a", p=P)).then_inc(ld_small, 16)
            act.dma_start(wx, W_x.rearrange("(k p) m -> p k m", p=P)).then_inc(ld_small, 16)
            act.dma_start(wfx[:, :, :], W_fx.rearrange("(k p) m -> p k m", p=P)).then_inc(ld_small, 16)
            act.dma_start(wout[:, :, :], W_out.rearrange("(a p) m -> p a m", p=P)).then_inc(ld_small, 16)
            n += 7
            assert n == SMALL_LOADS
            for a in range(HP):
                act.wait_ge(wxT_mm, a + 1)
                if a:
                    act.wait_ge(wlog_mm, a)
                nc.scalar.copy(wxT, bank["tr"][:, 0:D]).then_inc(wxT_saved, 1)

            def split(tile, j, send):
                for c in range(CH):
                    if send:
                        act.wait_ge(part_sent[c], tile * 16)
                    elif c == 0:
                        with act.If(j > 0):
                            for cc in range(CH):
                                act.wait_ge(part_sent[cc], j * 16)
                            alone(act)
                    act.wait_ge(chunk_mm, tile * CH + c + 1)
                    p3 = parts[:, c, :, :, :]
                    nc.scalar.copy(p3[:, :, 0, :], chunk[c % 2][:, :].rearrange("p (r d) -> p r d", r=2)).then_inc(hi_ready, 1)
                    act.wait_ge(res_ready, tile * CH + c + 1 + 2)
                    nc.scalar.copy(p3[:, :, 1, :], resid[:, c % 2, :].rearrange("p (r d) -> p r d", r=2)).then_inc(mid_ready, 1)
                    if send:
                        act.wait_ge(lo_ready, tile * CH + c + 1)
                        act.dma_start(msg_tiles[1][bass.ds(j, 1), :, c * 2 * ROW:(c + 1) * 2 * ROW].rearrange("a p d -> (a p) d"),
                                      p3.rearrange("p r h d -> p (r h d)")).then_inc(part_sent[c], 16)

            with act.Fori(0, NT) as j:
                act.wait_ge(var_ready, j + 1)
                nc.scalar.activation(std[:, 0, :], mv[:, 0, 1:2], ACT.Sqrt, bias=eps[:, :], scale=1.0).then_inc(std_ready, 1)
                act.wait_ge(tr_done, j + 1)
                nc.scalar.copy(xT[:, 0, :, :].rearrange("p k n -> p (k n)"), bank["tr"][:, 0:D]).then_inc(xT_ready, 1)
                split(j, j, False)
            act.dma_start(xin[:, 0, :], x[0:P, :]).then_inc(xin_full[0], 16)

            def hidden(j):
                act.wait_ge(tr_done, j + NT + 1)
                nc.scalar.copy(xT[:, 0, :, :].rearrange("p k n -> p (k n)"), bank["tr"][:, 0:D]).then_inc(xT_ready, 1)
                split(j + NT, j, True)
                act.wait_ge(base_ready, j + 1)

            with act.Fori(0, NT - 2) as j:
                hidden(j)
                act.dma_start(xin[:, 0, :], x[bass.ds((j + 1) * P, P), :]).then_inc(xin_full[0], 16)
            hidden(NT - 2)
            act.dma_start(xin[0:TAIL, 0, :], x[N - TAIL:N, :]).then_inc(xin_full[0], 16)
            hidden(NT - 1)
            act.dma_start(b1_bo[:, :], b_out.rearrange("(a n) -> a n", a=1).to_broadcast([P, D])).then_inc(ld_bo, 16)
            act.sem_inc(swT_saved, 1)
            with act.Fori(0, NT) as j:
                act.wait_ge(var_ready, j + NT + 1)
                nc.scalar.activation(std[:, 0, :], mv[:, 0, 1:2], ACT.Sqrt, bias=eps[:, :], scale=1.0).then_inc(std_ready, 1)
                act.wait_ge(tr_done, j + 2 * NT + 1)
                nc.scalar.copy(xT[:, 0, :, :].rearrange("p k n -> p (k n)"), bank["tr"][:, 0:D]).then_inc(xT_ready, 1)
                act.wait_ge(logit_ready, j + 1)
                nc.scalar.activation(logit[:, :], logit[:, :], ACT.Exp).then_inc(exp_ready, 1)
                act.wait_ge(swT_done, j + 1)
                nc.scalar.copy(swT[:, :, bass.ds(j * P, P)], chunk[1][:, :].rearrange("p (a n) -> p a n", a=HP)).then_inc(swT_saved, 1)
            act.wait_ge(qkv_mm, 1)
            for n3, name in enumerate(("agg", "tr", "self")):
                nc.scalar.copy(qkvT[n3], bank[name][:, 0:HP * G].rearrange("p (a g) -> p a g", a=HP)).then_inc(qkv_saved, 1)
            act.wait_ge(score_ready, 1)
            nc.scalar.activation(att, att, ACT.Exp, scale=SCALE).then_inc(score_exp, 1)
            act.wait_ge(vo_mm, 1)
            for h2 in range(2):
                for half in range(2):
                    nc.scalar.copy(vo[0:G, 4 * half + h2:4 * half + h2 + 3:2, :],
                                   bank[VO_BANKS[2 * h2 + half]][0:G, :].rearrange("p (h d) -> p h d", h=2)).then_inc(vo_saved, 1)
            act.wait_ge(mix_mm, 1)
            for half, name in enumerate(MIX_BANKS):
                nc.scalar.copy(mix[:, 2 * half:2 * half + 2, :], bank[name][:, :].rearrange("p (a d) -> p a d", a=2)).then_inc(mix_saved, 1)
            with act.Fori(0, NT // 2) as jj:
                for par in range(2):
                    j = jj * 2 + par
                    act.wait_ge(out_mm, j + 1)
                    nc.scalar.copy(swTile[:, par, :, :], swT[:, :, bass.ds(j * P, P)]).then_inc(tile_copied, 1)

        @block.vector
        def _(dve):
            ch = Chain(dve, dve_prep)
            dve.wait_ge(ld_edges, 16 * EDGE_LOADS)
            dve.wait_ge(consts_set, 1)
            ch.done(nc.vector.tensor_scalar(out=lo_i, in0=dst_t[:, :, 0], scalar1=7, scalar2=None, op0=ALU.logical_shift_right))
            nc.vector.memset(lo_i[0:1, 0:1], 0)
            ch.done(nc.vector.tensor_scalar(out=hi_i, in0=nxt_t, scalar1=7, scalar2=None, op0=ALU.logical_shift_right))
            ch.done(nc.vector.tensor_tensor(out=start_lo, in0=lo_i, in1=tile_no, op=ALU.add))
            ch.done(nc.vector.scalar_tensor_tensor(out=start_hi, in0=hi_i, scalar=1.0, in1=tile_no, op0=ALU.add, op1=ALU.add))
            for c in range(EC):
                nc.vector.tensor_scalar(out=ge_lo[:, c, :], in0=step_no, scalar1=start_lo[:, c:c + 1], scalar2=None, op0=ALU.is_ge)
                ch.done(nc.vector.tensor_scalar(out=ge_hi[:, c, :], in0=step_no, scalar1=start_hi[:, c:c + 1], scalar2=None, op0=ALU.is_ge))
            nc.vector.tensor_tensor(out=ge_hi, in0=ge_lo, in1=ge_hi, op=ALU.subtract)
            nc.vector.scalar_tensor_tensor(out=row_f, in0=src_t, scalar=float(R), in1=rel_t, op0=ALU.mult, op1=ALU.add)
            nc.vector.tensor_copy(dst_f, dst_t).then_inc(edges_ready, 1)
            dve.wait_ge(step_mm, 1)
            ch.done(nc.vector.scalar_tensor_tensor(out=nt_of, in0=step_no, scalar=1.0, in1=bank["agg"][:, 0:STEPS], op0=ALU.add, op1=ALU.subtract))
            nc.vector.tensor_copy(idx[:, :], bank["self"][:, 0:STEPS])
            nc.vector.scalar_tensor_tensor(out=seg[:, :], in0=nt_of, scalar=-float(P), in1=bank["misc"][:, 0:STEPS],
                                           op0=ALU.mult, op1=ALU.add)
            ch.done(nc.vector.tensor_scalar(out=le, in0=nt_of, scalar1=part_no, scalar2=None, op0=ALU.is_le))
            nc.vector.tensor_reduce(out=endc, in_=le, axis=AX.X, op=ALU.add).then_inc(endc_ready, 1)
            dve.wait_ge(ends_mm, 1)
            ch.done(nc.vector.tensor_scalar(out=ends[:, :], in0=bank["tr"][0:1, 0:P], scalar1=-1.0, scalar2=None, op0=ALU.add))
            nc.vector.memset(ends[0:1, NT:], 1 << 20).then_inc(ends_ready, 1)
            dve.wait_ge(ld_small, 16 * SMALL_LOADS)
            ch.done(nc.vector.tensor_scalar(out=itemp, in0=temp_all, scalar1=0.1, scalar2=5.0, op0=ALU.max, op1=ALU.min))
            ch.done(nc.vector.reciprocal(itemp, itemp))
            nc.vector.tensor_copy(bx_all, bx_col[:, :].rearrange("p (a n) -> p a n", n=1).to_broadcast([P, HP, P])).then_inc(bx_ready, 1)
            for a in range(HP):
                dve.wait_ge(wlog_mm, a + 1)
                pair = slice(a * P, (a + 1) * P)
                two = itemp[:, 2 * a:2 * a + 2].rearrange("p (h g) -> p h g", g=1).to_broadcast([P, 2, G])
                for k in range(K2):
                    nc.vector.tensor_tensor(out=heads(wlog[:, k, pair]), in0=heads(chunk[0][:, k * P:(k + 1) * P]), in1=two, op=ALU.mult)
                ch.done(nc.vector.tensor_tensor(out=heads(blog[:, pair]), in0=heads(chunk[0][:, 2 * P:3 * P]),
                                        in1=bsl.rearrange("p (a g) -> p a g", a=1).to_broadcast([P, 2, G]), op=ALU.add))
                nc.vector.tensor_tensor(out=heads(blog[:, pair]), in0=heads(blog[:, pair]), in1=two, op=ALU.mult).then_inc(wlog_saved, 1)
            nc.vector.sem_inc(res_ready, 2)
            nc.vector.sem_inc(self_free, 1)
            dve.wait_ge(wlog_saved, HP)

            def norm(c, rows, n, par):
                alone(dve)
                c.done(nc.vector.bn_stats(stats[:, :], rows))
                alone(dve)
                ins = nc.vector.bn_aggr(mv[:, 0, :], stats[:, :])
                ins.then_inc(var_ready, 1)
                dve.wait_ge(std_ready, n + 1)
                c.done(nc.vector.reciprocal(rstd[:, 0, :], std[:, 0, :]))
                return nc.vector.tensor_scalar(out=xn[:, par, :], in0=rows, scalar1=mv[:, 0, 0:1], scalar2=rstd[:, 0, :],
                                               op0=ALU.subtract, op1=ALU.mult)

            def split(tile):
                for c in range(CH):
                    p3 = parts[:, c, :, :, :]
                    left = resid[:, c % 2, :].rearrange("p (r d) -> p r d", r=2)
                    dve.wait_ge(hi_ready, tile * CH + c + 1)
                    nc.vector.tensor_tensor(out=left, in0=chunk[c % 2][:, :].rearrange("p (r d) -> p r d", r=2),
                                            in1=p3[:, :, 0, :], op=ALU.subtract).then_inc(res_ready, 1)
                    dve.wait_ge(mid_ready, tile * CH + c + 1)
                    nc.vector.tensor_tensor(out=p3[:, :, 2, :], in0=left, in1=p3[:, :, 1, :], op=ALU.subtract).then_inc(lo_ready, 1)

            def one_hots(g):
                nc.vector.tensor_tensor(
                    out=onehot[:, bass.ds(g * RING, RING), :],
                    in0=node_no[:, :].rearrange("p (a n) -> p a n", a=1).to_broadcast([P, RING, P]),
                    in1=seg[:, bass.ds(g * RING, RING)].rearrange("p (s a) -> p s a", a=1).to_broadcast([P, RING, P]),
                    op=ALU.is_equal).then_inc(onehot_ready, 1)

            with dve.Fori(0, NT // 2) as jj:
                c = Chain(dve, norm1_steps, jj, 4)
                for par in range(2):
                    j = jj * 2 + par
                    dve.wait_ge(xin_full[par], (jj + 1) * 16)
                    norm(c, xin[:, par, :], j, par).then_inc(xn_ready, 1)
                    dve.wait_ge(self_mm, j + 1)
                    nc.vector.tensor_tensor(out=tile_at(base, j), in0=bank["self"][:, 0:D], in1=b1_bo[:, :], op=ALU.add).then_inc(self_free, 1)
                    split(j)
                    one_hots(j)
                assert c.n == 4
            for g in range(NT, GROUPS):
                one_hots(g)

            with dve.Fori(0, NT) as j:
                dve.wait_ge(agg_done, j + 1)
                nc.vector.tensor_tensor(out=xn[:, 0, :], in0=agg, in1=tile_at(base, j), op=ALU.add).then_inc(agg_free, 1)
                dve.wait_ge(agg_free, j + 1)
                nc.vector.tensor_scalar(out=xn[:, 0, :], in0=xn[:, 0, :], scalar1=0.0, scalar2=None, op0=ALU.max).then_inc(xn_ready, 1)
                dve.wait_ge(self_mm, j + NT + 1)
                dve.wait_ge(xin_full[0], (j + NT // 2 + 1) * 16)
                nc.vector.tensor_tensor(out=tile_at(base, j), in0=bank["self"][:, 0:D], in1=xin[:, 0, :], op=ALU.add).then_inc(self_free, 1)
                dve.wait_ge(self_free, j + NT + 2)
                nc.vector.tensor_tensor(out=tile_at(base, j), in0=tile_at(base, j), in1=b2_all[:, :], op=ALU.add).then_inc(base_ready, 1)
                split(j + NT)

            with dve.Fori(0, NT) as j:
                c = Chain(dve, slice_steps, j, 7)
                rows = tile_at(base, j)
                dve.wait_ge(agg_done, j + NT + 1)
                nc.vector.tensor_tensor(out=rows, in0=agg, in1=rows, op=ALU.add).then_inc(agg_free, 1)
                dve.wait_ge(agg_free, j + NT + 1)
                norm(c, rows, j + NT, 0).then_inc(xn_ready, 1)
                dve.wait_ge(logit_mm, j + 1)
                c.done(nc.vector.tensor_tensor(out=logit[:, :], in0=chunk[0][:, :], in1=blog[:, :], op=ALU.add))
                c.done(nc.vector.tensor_reduce(out=hmax[:, :], in_=heads(logit[:, :]), axis=AX.X, op=ALU.max))
                nc.vector.tensor_tensor(out=heads(logit[:, :]), in0=heads(logit[:, :]),
                                        in1=hmax[:, :].rearrange("p (h g) -> p h g", g=1).to_broadcast([P, H, G]),
                                        op=ALU.subtract).then_inc(logit_ready, 1)
                dve.wait_ge(exp_ready, j + 1)
                c.done(nc.vector.tensor_reduce(out=hsum[:, :], in_=heads(logit[:, :]), axis=AX.X, op=ALU.add))
                c.done(nc.vector.reciprocal(hsum[:, :], hsum[:, :]))
                c.done(nc.vector.tensor_scalar(out=hsum[:, :], in0=hsum[:, :], scalar1=mask[:, bass.ds(j, 1)], scalar2=None, op0=ALU.mult))
                nc.vector.tensor_tensor(out=heads(sw[:, :]), in0=heads(logit[:, :]),
                                        in1=hsum[:, :].rearrange("p (h g) -> p h g", g=1).to_broadcast([P, H, G]),
                                        op=ALU.mult).then_inc(sw_ready, 1)
                dve.wait_ge(sw_ready, j + 1)
                nc.vector.tensor_tensor(out=swsum[:, :], in0=swsum[:, :], in1=sw[:, :], op=ALU.add).then_inc(swsum_steps, 1)
                assert c.n == 7

            ch = Chain(dve, tail_steps)
            dve.wait_ge(norm_mm, 1)
            nrm = bank["misc"][:, :]
            ch.done(nc.vector.tensor_scalar(out=rnorm, in0=nrm, scalar1=EPS_SLICE, scalar2=None, op0=ALU.add))
            ch.done(nc.vector.reciprocal(rnorm, rnorm))
            for m in range(K2):
                nc.vector.tensor_tensor(out=ttn[:, m, :], in0=bank[f"t{m}"][:, :], in1=rnorm, op=ALU.mult).then_inc(ttn_ready, 1)
            ch.done(nc.vector.tensor_tensor(out=cnorm, in0=nrm, in1=rnorm, op=ALU.mult))
            for h2 in range(2):
                rows = slice(h2 * C, (h2 + 1) * C)
                ch.done(nc.vector.tensor_tensor(
                    out=tokC[rows, :, :], in0=cnorm[rows, :].rearrange("p (a n) -> p a n", a=HP)[:, :, h2 * G:(h2 + 1) * G],
                    in1=bfx_col[rows, :].rearrange("p (a n) -> p a n", n=1).to_broadcast([C, HP, G]), op=ALU.mult))
            dve.wait_ge(tok_mm, 1)
            for h2 in range(2):
                rows = slice(h2 * C, (h2 + 1) * C)
                nc.vector.tensor_tensor(
                    out=tokC[rows, :, :], in0=tokC[rows, :, :],
                    in1=bank["c0"][rows, :].rearrange("p (a n) -> p a n", a=HP)[:, :, h2 * G:(h2 + 1) * G],
                    op=ALU.add).then_inc(tok_ready, 1)
            dve.wait_ge(score_mm, 1)
            for h2 in range(2):
                rows = slice(h2 * G, (h2 + 1) * G)
                s3 = bank[f"t{h2}"][rows, 0:HP * G].rearrange("p (a g) -> p a g", a=HP)
                ch.done(nc.vector.tensor_reduce(out=amax[rows, :], in_=s3, axis=AX.X, op=ALU.max))
                ch.done(nc.vector.tensor_tensor(out=att[rows, :, :], in0=s3,
                                                in1=amax[rows, :].rearrange("p (a n) -> p a n", n=1).to_broadcast([G, HP, G]), op=ALU.subtract))
            nc.vector.sem_inc(score_ready, 1)
            dve.wait_ge(score_exp, 1)
            ch.done(nc.vector.tensor_reduce(out=asum, in_=att, axis=AX.X, op=ALU.add))
            ch.done(nc.vector.reciprocal(asum, asum))
            nc.vector.tensor_tensor(out=att, in0=att, in1=asum.rearrange("p (a n) -> p a n", n=1).to_broadcast([P, HP, G]),
                                    op=ALU.mult).then_inc(att_ready, 1)
            dve.wait_ge(attT_mm, 1)
            nc.vector.tensor_copy(attT[0:G, :, :], bank["misc"][0:G, :].rearrange("p (a n) -> p a n", a=HP)).then_inc(attT_saved, 1)
            dve.wait_ge(ld_bo, 16)
            nc.vector.sem_inc(out_added, 2)
            with dve.Fori(0, NT // 2) as jj:
                for par in range(2):
                    j = jj * 2 + par
                    with dve.If(jj > 0):
                        dve.wait_ge(res_sent[par], jj * 16)
                        alone(dve)
                    dve.wait_ge(out_mm, 2 + j + 1)
                    nc.vector.tensor_tensor(out=res[:, par, :], in0=bank[f"c{par}"][:, 0:D], in1=tile_at(base, j), op=ALU.add).then_inc(out_added, 1)
                    dve.wait_ge(out_added, j + 3)
                    nc.vector.tensor_tensor(out=res[:, par, :], in0=res[:, par, :], in1=b1_bo[:, :], op=ALU.add).then_inc(out_ready, 1)

        @block.tensor
        def _(pe):
            mm = nc.tensor.matmul
            pe.wait_ge(consts_set, 1)
            pe.wait_ge(edges_ready, 1)
            for lhsT, rhs, to in ((None, ge_lo, "agg"), (row_f, ge_hi, "self"), (dst_f, ge_hi, "misc")):
                for c in range(EC):
                    last = mm(bank[to][:, 0:STEPS], ones[:, :] if lhsT is None else lhsT[:, c, :], rhs[:, c, :],
                              start=(c == 0), stop=(c == EC - 1))
            last.then_inc(step_mm, 1)
            pe.wait_ge(endc_ready, 1)
            mm(bank["tr"][0:1, 0:P], endc, ident[:, :], start=True, stop=True).then_inc(ends_mm, 1)
            pe.wait_ge(ends_ready, 1)
            pe.wait_ge(bx_ready, 1)
            for a in range(HP):
                pair = slice(a * P, (a + 1) * P)
                if a:
                    pe.wait_ge(wxT_saved, a)
                for k in range(K2):
                    last = nc.tensor.transpose(bank["tr"][:, k * P:(k + 1) * P], wx[:, k, pair], ident[:, :])
                last.then_inc(wxT_mm, 1)
                pe.wait_ge(wxT_saved, a + 1)
                if a:
                    pe.wait_ge(wlog_saved, a)
                for k in range(K2):
                    mm(chunk[0][:, k * P:(k + 1) * P], wxT[:, k * P:(k + 1) * P], bd["s"][:, :], start=True, stop=True)
                mm(chunk[0][:, 2 * P:3 * P], bx_all[:, a, :], bd["s"][:, :], start=True, stop=True).then_inc(wlog_mm, 1)

            def transform(tile, par):
                pe.wait_ge(xn_ready, tile + 1)
                for k in range(K2):
                    last = nc.tensor.transpose(bank["tr"][:, k * P:(k + 1) * P], xn[:, par, k * P:(k + 1) * P], ident[:, :])
                last.then_inc(tr_done, 1)
                pe.wait_ge(xT_ready, tile + 1)
                pe.wait_ge(self_free, tile + 1)
                for k in range(K2):
                    last = mm(bank["self"][:, 0:D], xT[:, 0, k, :], wself[:, k, :], start=(k == 0), stop=(k == K2 - 1))
                last.then_inc(self_mm, 1)
                for c in range(CH):
                    pe.wait_ge(res_ready, tile * CH + c + 1)
                    for k in range(K2):
                        last = mm(chunk[c % 2][:, :], xT[:, 0, k, :], wrel[:, k, c * CW:(c + 1) * CW], start=(k == 0), stop=(k == K2 - 1))
                    last.then_inc(chunk_mm, 1)

            pe.wait_ge(wlog_saved, HP)
            pe.wait_ge(ld_w1, 16 * (K2 + 1))
            with pe.Fori(0, NT // 2) as jj:
                for par in range(2):
                    transform(jj * 2 + par, par)

            def clear(out):
                return mm(out, zeros[:, 0:P], zeros[:, :], start=True, stop=True, skip_group_check=True)

            def slices(t):
                pe.wait_ge(xn_ready, t + 2 * NT + 1)
                for k in range(K2):
                    last = nc.tensor.transpose(bank["tr"][:, k * P:(k + 1) * P], xn[:, 0, k * P:(k + 1) * P], ident[:, :])
                last.then_inc(tr_done, 1)
                pe.wait_ge(xT_ready, t + 2 * NT + 1)
                for k in range(K2):
                    last = mm(chunk[0][:, :], xT[:, 0, k, :], wlog[:, k, :], start=(k == 0), stop=(k == K2 - 1))
                last.then_inc(logit_mm, 1)
                pe.wait_ge(sw_ready, t + 1)
                for m in range(K2):
                    mm(bank[f"t{m}"][:, :], xn[:, 0, m * P:(m + 1) * P], sw[:, :], start=False, stop=True, skip_group_check=True)
                pe.wait_ge(swT_saved, t + 1)
                for a in range(HP):
                    last = nc.tensor.transpose(chunk[1][:, a * P:(a + 1) * P], sw[:, a * P:(a + 1) * P], ident[:, :])
                last.then_inc(swT_done, 1)

            tile = pe.alloc_register("tile")
            end = pe.alloc_register("end")
            pe.sem_inc(ring_free, RING)
            pe.wait_ge(onehot_ready, GROUPS)
            clear(agg)
            for layer in range(2):
                pe.reg_mov(tile, 0)
                pe.reg_mov(end, pe.value_load(ends[0:1, 0:1]))
                if layer:
                    pe.wait_ge(self_free, 2 * NT + 1)
                    for m in range(K2):
                        mm(bank[f"t{m}"][:, :], zeros[:, 0:P], onehot[:, 0:4, :].rearrange("p s n -> p (s n)"),
                           start=True, stop=True, skip_group_check=True)
                with pe.Fori(0, GROUPS) as g:
                    with pe.Fori(0, RING) as i:
                        s = g * RING + i
                        pe.wait_ge(rows_ready, s + layer * STEPS + 1)
                        for part in range(3):
                            last = mm(agg, onehot[:, bass.ds(s, 1), :].rearrange("p a n -> p (a n)"),
                                      ring[:, bass.ds(i, 1), part * D:(part + 1) * D].rearrange("p a n -> p (a n)"),
                                      start=False, stop=True, skip_group_check=True)
                        last.then_inc(ring_free, 1)
                        with pe.If(pe.snap(end) == s):
                            mm(agg, zeros[:, 0:P], zeros[:, :], start=False, stop=True, skip_group_check=True).then_inc(agg_done, 1)
                            t = pe.snap(tile, min_val=0, max_val=NT - 1)
                            pe.wait_ge(agg_free, t + layer * NT + 1)
                            clear(agg)
                            if layer == 0:
                                pe.wait_ge(ld_w2, 16 * (K2 + 1))
                                transform(t + NT, 0)
                            else:
                                slices(t)
                            pe.reg_add(tile, tile, 1)
                            t2 = pe.snap(tile, min_val=0, max_val=NT)
                            pe.reg_mov(end, pe.value_load(ends[0:1, bass.ds(t2, 1)]))

            pe.wait_ge(swsum_steps, NT)
            mm(bank["misc"][:, :], ones[:, :], swsum[:, :], start=True, stop=True).then_inc(norm_mm, 1)
            pe.wait_ge(ttn_ready, K2)
            for a in range(HP):
                pair = slice(a * P, (a + 1) * P)
                for k in range(K2):
                    last = mm(bank["c0"][:, pair], wfx[:, k, pair], ttn[:, k, pair], start=(k == 0), stop=(k == K2 - 1))
            last.then_inc(tok_mm, 1)
            pe.wait_ge(tok_ready, 2)
            tok = tokC.rearrange("p a g -> p (a g)")
            for name, to in (("q", "agg"), ("k", "tr"), ("v", "self")):
                last = mm(bank[to][:, 0:HP * G], bd[name][:, :], tok, start=True, stop=True)
            last.then_inc(qkv_mm, 1)
            pe.wait_ge(qkv_saved, 3)
            qT, kT, vT = qkvT
            for h2 in range(2):
                rows = slice(h2 * G, (h2 + 1) * G)
                for a in range(HP):
                    last = mm(bank[f"t{h2}"][rows, a * G:(a + 1) * G], qT[rows, a, :], kT[rows, a, :], start=True, stop=True)
            last.then_inc(score_mm, 1)
            for h2 in range(2):
                rows = slice(h2 * G, (h2 + 1) * G)
                for a in range(HP):
                    last = mm(bank[VO_BANKS[2 * h2 + a // 2]][0:G, (a % 2) * D:(a % 2 + 1) * D], vT[rows, a, :], wout[rows, a, :], start=True, stop=True)
            last.then_inc(vo_mm, 1)
            pe.wait_ge(att_ready, 1)
            for a in range(HP):
                last = nc.tensor.transpose(bank["misc"][0:G, a * P:(a + 1) * P], att[:, a, :], ident[:, :])
            last.then_inc(attT_mm, 1)
            pe.wait_ge(attT_saved, 1)
            pe.wait_ge(vo_saved, 4)
            for h2 in range(2):
                rows = slice(h2 * G, (h2 + 1) * G)
                for a in range(HP):
                    last = mm(bank[MIX_BANKS[a // 2]][rows, (a % 2) * D:(a % 2 + 1) * D], attT[0:G, a, rows], vo[0:G, 2 * a + h2, :], start=True, stop=True)
            last.then_inc(mix_mm, 1)
            pe.wait_ge(mix_saved, 2)
            pe.sem_inc(out_mm, 2)
            with pe.Fori(0, NT // 2) as jj:
                for par in range(2):
                    j = jj * 2 + par
                    pe.wait_ge(tile_copied, j + 1)
                    pe.wait_ge(out_added, j + 1)
                    for a in range(HP):
                        last = mm(bank[f"c{par}"][:, 0:D], swTile[:, par, a, :], mix[:, a, :], start=(a == 0), stop=(a == HP - 1))
                    last.then_inc(out_mm, 1)


_INS = ['x', 'src', 'dst', 'edge_type_8', 'L0_gnn_W1', 'L0_gnn_self_w1', 'L0_gnn_b1', 'L0_gnn_W2', 'L0_gnn_self_w2', 'L0_gnn_b2',
        'L0_ffn_W_fx', 'L0_ffn_b_fx', 'L0_ffn_W_x', 'L0_ffn_b_x', 'L0_ffn_W_slice', 'L0_ffn_b_slice', 'L0_ffn_W_q', 'L0_ffn_W_k',
        'L0_ffn_W_v', 'L0_ffn_W_out', 'L0_ffn_b_out', 'L0_ffn_temperature']


def kernel(**inputs):
    import concourse.bacc as bacc
    from concourse.bass_utils import run_bass_kernel_spmd

    nc = bacc.Bacc("TRN2", target_bir_lowering=False, num_devices=1)
    arrays, args = {}, []
    for name in _INS:
        a = np.ascontiguousarray(inputs[name])
        arrays[f"in_{name}"] = a
        args.append(nc.dram_tensor(f"in_{name}", a.shape, mybir.dt.from_np(a.dtype), kind="ExternalInput").ap())
    out = nc.dram_tensor("out", (N, D), f32, kind="ExternalOutput").ap()
    rgcn_slice_attention(nc, *args, out)
    r = run_bass_kernel_spmd(nc, [arrays], core_ids=[0])
    return r.results[0]["out"]
```

```python
import concourse.bass as bass
from concourse import mybir
from contextlib import ExitStack
import numpy as np

f32 = mybir.dt.float32
bf16 = mybir.dt.bfloat16
i32 = mybir.dt.int32
u32 = mybir.dt.uint32
ALU = mybir.AluOpType
ACT = mybir.ActivationFunctionType
AX = mybir.AxisListType

P = 128
N, E, D, R = 2500, 40000, 256, 8
K2 = D // P
NT = -(-N // P)
TAIL = N - (NT - 1) * P
ET = -(-E // P)
EC = -(-ET // P)
RING = 16
HALF = RING // 2
STEPS = -(-(ET + NT - 1) // RING) * RING
GROUPS = STEPS // RING
ROW = 3 * D
CH = 4
CW = R * D // CH
H, C, G = 8, 64, 64
HP = H // 2
HG = H * G
EPS_LN = 1e-5
EPS_SLICE = 1e-5
SCALE = float(C) ** -0.5
NO_NODE = 4096


class Chain:

    def __init__(self, eng, sem, it=0, per_turn=0):
        self.eng, self.sem, self.base, self.n = eng, sem, it * per_turn, 0

    def done(self, ins):
        self.n += 1
        ins.then_inc(self.sem, 1)
        self.eng.wait_ge(self.sem, self.base + self.n)


def rgcn_slice_attention(nc, x, src, dst, rel, W1, self_w1, b1, W2, self_w2, b2, W_fx, b_fx, W_x, b_x,
                         W_slice, b_slice, W_q, W_k, W_v, W_out, b_out, temperature, out):
    msg1 = nc.dram_tensor("msg1", (NT * P * R, ROW), bf16, kind="Internal").ap()
    msg2 = nc.dram_tensor("msg2", (NT * P * R, ROW), bf16, kind="Internal").ap()
    msg_tiles = [m.rearrange("(t p r) d -> t p (r d)", p=P, r=R) for m in (msg1, msg2)]

    with ExitStack() as ctx:
        ctx.enter_context(nc.allow_non_contiguous_dma(reason="a few small columns of biases and indices"))
        sb = lambda name, shape, dt=f32: ctx.enter_context(nc.sbuf_tensor(name, shape, dt))
        sem = lambda name: ctx.enter_context(nc.semaphore(name))

        onehot = sb("onehot", [P, STEPS, P], bf16)
        ring = sb("ring", [P, RING, ROW], bf16)
        base = sb("base", [P, NT, D])
        area = sb("area", [P, HP * NT * P])
        wrel = area[:, 0:K2 * R * D].rearrange("p (k m) -> p k m", k=K2)
        o = K2 * R * D
        parts = area[:, o:o + CH * 2 * ROW // 2].bitcast(bf16).rearrange("p (c r h d) -> p c r h d", c=CH, r=2, h=3)
        o += CH * 2 * ROW // 2
        resid = area[:, o:o + 2 * CW].rearrange("p (b m) -> p b m", b=2)
        swT = area[:, :].rearrange("p (a n) -> p a n", a=HP)
        idx = sb("idx", [P, STEPS], i32)
        idx_now = sb("idx_now", [P, RING], u32)
        seg = sb("seg", [P, STEPS])
        wself = sb("wself", [P, K2, D])
        wfx = sb("wfx", [P, K2, HG])
        wlog = sb("wlog", [P, K2, HG])
        wout = sb("wout", [P, HP, D])
        b1_bo = sb("b1_bo", [P, D])
        b2_all = sb("b2_all", [P, D])
        blog = sb("blog", [P, HG])
        xin = sb("xin", [P, 2, D])
        xn = sb("xn", [P, 2, D])
        xT = sb("xT", [P, 2, K2, P])
        logit = sb("logit", [P, HG])
        sw = sb("sw", [P, HG])
        swsum = sb("swsum", [P, HG])
        ident = sb("ident", [P, P])
        ones = sb("ones", [P, P])
        zeros = sb("zeros", [P, D], bf16)
        bd = {n: sb(f"bd_{n}", [P, P]) for n in ("s", "q", "k", "v")}
        bfx_col = sb("bfx_col", [P, HP])
        bx_col = sb("bx_col", [P, HP])
        ends = sb("ends", [1, P], i32)
        eps = sb("eps", [P, 1])
        mask = sb("mask", [P, NT])
        stats = sb("stats", [P, 6])
        mv = sb("mv", [P, 2, 2])
        std = sb("std", [P, 2, 1])
        rstd = sb("rstd", [P, 2, 1])
        hmax = sb("hmax", [P, H])
        hsum = sb("hsum", [P, H])

        ringf = ring[:, :, :].rearrange("p s d -> p (s d)").bitcast(f32)
        ringi = ring[:, :, :].rearrange("p s d -> p (s d)").bitcast(i32)
        at = [0]

        def cut(view, *dims):
            n = int(np.prod(dims))
            got = view[:, at[0]:at[0] + n]
            at[0] += n
            return got.rearrange("p (a b) -> p a b", a=dims[0]) if len(dims) == 2 else got

        src_t, dst_t, rel_t = (cut(ringi, EC, P) for _ in range(3))
        nxt_t, lo_i, hi_i = (cut(ringi, EC) for _ in range(3))
        tile_no = cut(ringf, EC)
        start_lo, start_hi = cut(ringf, EC), cut(ringf, EC)
        row_f, dst_f = cut(ringf, EC, P), cut(ringf, EC, P)
        ge_lo, ge_hi = cut(ringf, EC, STEPS), cut(ringf, EC, STEPS)
        step_no = cut(ringf, STEPS)
        nt_of = cut(ringf, STEPS)
        endc = cut(ringf, 1)
        part_no = cut(ringf, 1)
        assert at[0] <= RING * ROW // 2
        ohf = onehot[:, :, :].rearrange("p s n -> p (s n)").bitcast(f32)
        wx = ohf[:, 0:K2 * HG].rearrange("p (k m) -> p k m", k=K2)
        wxT = ohf[:, 1024:1024 + D]
        bx_all = ohf[:, 1536:1536 + P * HP].rearrange("p (a n) -> p a n", a=HP)
        temp_all = ohf[:, 2048:2048 + H]
        itemp = ohf[:, 2064:2064 + H]
        bsl = ohf[:, 2080:2080 + G]
        le = ohf[:, 2304:2304 + STEPS]
        node_no = sb("node_no", [P, P], bf16)
        at[0] = 0
        ttn = cut(ringf, K2, HG)
        rnorm = cut(ringf, HG)
        cnorm = cut(ringf, HG)
        tokC = cut(ringf, HP, G)
        qkvT = [cut(ringf, HP, G) for _ in range(3)]
        att = cut(ringf, HP, G)
        attT = cut(ringf, HP, P)
        vo = cut(ringf, H, D)
        amax, asum = cut(ringf, HP), cut(ringf, HP)
        assert at[0] <= RING * ROW // 2
        mix = onehot[:, 0:16, :].rearrange("p s n -> p (s n)").bitcast(f32).rearrange("p (a d) -> p a d", a=HP)
        swTile = onehot[:, 16:32, :].rearrange("p s n -> p (s n)").bitcast(f32).rearrange("p (b a n) -> p b a n", b=2, a=HP)
        res = onehot[:, 32:48, :].rearrange("p s n -> p (s n)").bitcast(f32)[:, 0:2 * D].rearrange("p (b d) -> p b d", b=2)

        bank = {n: ctx.enter_context(nc.psum_tensor(n, [P, 512], f32))
                for n in ("tr", "self", "c0", "c1", "t0", "t1")}
        agg2 = ctx.enter_context(nc.psum_tensor("agg2", [P, 2 * 512], f32))
        bank["agg0"], bank["agg1"] = agg2[:, 0:512], agg2[:, 512:1024]
        aggs, chunk = [agg2[:, 0:D], agg2[:, 512:512 + D]], [bank["c0"], bank["c1"]]

        xin_full = [sem("xin_full0"), sem("xin_full1")]
        part_sent = [sem(f"part_sent{c}") for c in range(CH)]
        slot_full = [sem(f"slot_full{i}") for i in range(RING)]
        res_sent = [sem("res_sent0"), sem("res_sent1")]
        names = """pads_set consts_set ld_edges ld_small ld_w1 ld_w2 ld_bo dve_prep edges_ready step_mm endc_ready
        ends_mm ends_ready bx_ready wxT_mm wxT_saved wlog_mm wlog_saved onehot_ready
        var_ready std_ready xn_ready tr_done xT_ready self_free self_mm chunk_mm hi_ready res_ready mid_ready lo_ready
        idx_copied rows_ready ring_free agg_done agg_free base_ready
        logit_mm logit_ready exp_ready sw_ready swT_done swT_saved
        norm1_steps norm2_steps prev_ready slice_steps swsum_steps tail_steps
        norm_mm ttn_ready tok_mm tok_ready qkv_mm qkv_saved score_mm score_ready score_exp att_ready attT_mm attT_saved
        vo_mm vo_saved mix_mm mix_saved tile_copied out_mm out_added out_ready""".split()
        sems = {name: sem(name) for name in names}
        (pads_set, consts_set, ld_edges, ld_small, ld_w1, ld_w2, ld_bo, dve_prep, edges_ready, step_mm, endc_ready,
         ends_mm, ends_ready, bx_ready, wxT_mm, wxT_saved, wlog_mm, wlog_saved, onehot_ready,
         var_ready, std_ready, xn_ready, tr_done, xT_ready, self_free, self_mm, chunk_mm, hi_ready, res_ready, mid_ready, lo_ready,
         idx_copied, rows_ready, ring_free, agg_done, agg_free, base_ready,
         logit_mm, logit_ready, exp_ready, sw_ready, swT_done, swT_saved,
         norm1_steps, norm2_steps, prev_ready, slice_steps, swsum_steps, tail_steps,
         norm_mm, ttn_ready, tok_mm, tok_ready, qkv_mm, qkv_saved, score_mm, score_ready, score_exp, att_ready, attT_mm, attT_saved,
         vo_mm, vo_saved, mix_mm, mix_saved, tile_copied, out_mm, out_added, out_ready) = (sems[name] for name in names)

        VO_BANKS, MIX_BANKS = ("agg0", "tr", "self", "c1"), ("t0", "t1")

        past = {e.engine: sem(f"past_{n}") for n, e in (("pool", nc.gpsimd), ("act", nc.scalar), ("dve", nc.vector))}

        def alone(eng):
            eng.sem_inc(past[eng.engine], 1)

        def tile_at(view, j):
            return view[:, bass.ds(j, 1), :].rearrange("p a n -> p (a n)")

        def heads(view):
            return view.rearrange("p (h g) -> p h g", g=G)

        block = ctx.enter_context(nc.Block())

        EDGE_LOADS, SMALL_LOADS = 4 * 3 + EC, 17

        @block.sync
        def _(sp):
            sp.wait_ge(pads_set, 1)
            whole = (E // P) * P
            for arr, t in ((dst, dst_t), (src, src_t), (rel, rel_t)):
                for c in range(EC):
                    lo, hi = c * P * P, min((c + 1) * P * P, whole)
                    sp.dma_start(t[0:(hi - lo) // P, c, :], arr[lo:hi].rearrange("(t e) -> t e", e=P)).then_inc(ld_edges, 16)
                r0 = whole // P - (EC - 1) * P
                sp.dma_start(t[r0:r0 + 1, EC - 1, 0:E - whole], arr[whole:E].rearrange("(t e) -> t e", t=1)).then_inc(ld_edges, 16)
            firsts = dst[P:E:P].rearrange("(t e) -> t e", e=1)
            for c in range(EC):
                m = min(P, ET - 1 - c * P)
                sp.dma_start(nxt_t[0:m, c:c + 1], firsts[c * P:c * P + m, :]).then_inc(ld_edges, 16)
            for par in range(2):
                sp.dma_start(xin[:, par, :], x[par * P:(par + 1) * P, :]).then_inc(xin_full[par], 16)
            for k in range(K2):
                sp.dma_start(wrel[:, k, :].rearrange("p (r m) -> p r m", r=R), W1[:, k * P:(k + 1) * P, :].rearrange("r p m -> p r m")).then_inc(ld_w1, 16)
            sp.dma_start(wself[:, :, :], self_w1.rearrange("(k p) m -> p k m", p=P)).then_inc(ld_w1, 16)

            def send_table(jj, full):
                for par in range(2):
                    j = jj * 2 + par
                    for c in range(CH):
                        sp.wait_ge(lo_ready, j * CH + c + 1)
                        sp.dma_start(msg_tiles[0][bass.ds(j, 1), :, c * 2 * ROW:(c + 1) * 2 * ROW].rearrange("a p d -> (a p) d"),
                                     parts[:, c, :, :, :].rearrange("p r h d -> p (r h d)")).then_inc(part_sent[c], 16)
                    if full:
                        sp.wait_ge(xn_ready, j + 1)
                    if par < full:
                        sp.dma_start(xin[:, par, :], x[bass.ds((j + 2) * P, P), :]).then_inc(xin_full[par], 16)
                    elif full:
                        sp.dma_start(xin[0:TAIL, par, :], x[N - TAIL:N, :]).then_inc(xin_full[par], 16)

            with sp.Fori(0, NT // 2 - 2) as jj:
                send_table(jj, 2)
            send_table(NT // 2 - 2, 1)
            send_table(NT // 2 - 1, 0)
            sp.wait_ge(chunk_mm, NT * CH)
            for k in range(K2):
                sp.dma_start(wrel[:, k, :].rearrange("p (r m) -> p r m", r=R), W2[:, k * P:(k + 1) * P, :].rearrange("r p m -> p r m")).then_inc(ld_w2, 16)
            sp.dma_start(wself[:, :, :], self_w2.rearrange("(k p) m -> p k m", p=P)).then_inc(ld_w2, 16)
            with sp.Fori(0, 2 * GROUPS) as g:
                for i in range(RING):
                    sp.wait_ge(slot_full[i], (g + 1) * 16)
                    sp.sem_inc(rows_ready, 1)
            with sp.Fori(0, NT // 2 - 1) as jj:
                for par in range(2):
                    sp.wait_ge(out_ready, jj * 2 + par + 1)
                    sp.dma_start(out[bass.ds((jj * 2 + par) * P, P), :], res[:, par, :]).then_inc(res_sent[par], 16)
            sp.wait_ge(out_ready, NT - 1)
            sp.dma_start(out[(NT - 2) * P:(NT - 1) * P, :], res[:, 0, :]).then_inc(res_sent[0], 16)
            sp.wait_ge(out_ready, NT)
            sp.dma_start(out[N - TAIL:N, :], res[0:TAIL, 1, :]).then_inc(res_sent[1], 16)
            for par in range(2):
                sp.wait_ge(res_sent[par], 16 * (NT // 2))

        @block.gpsimd
        def _(pool):
            nc.gpsimd.memset(dst_t, NO_NODE)
            nc.gpsimd.memset(src_t, 0)
            nc.gpsimd.memset(rel_t, 0)
            nc.gpsimd.memset(nxt_t, NO_NODE).then_inc(pads_set, 1)
            nc.gpsimd.memset(ones[:, :], 1.0)
            nc.gpsimd.memset(zeros[:, :], 0.0)
            nc.gpsimd.memset(swsum[:, :], 0.0)
            nc.gpsimd.memset(eps[:, :], EPS_LN)
            nc.gpsimd.memset(mask[:, :], 1.0)
            for m in bd.values():
                nc.gpsimd.memset(m[:, :], 0.0)
            nc.gpsimd.iota(tile_no, [[P, EC]], base=0, channel_multiplier=1, allow_small_or_imprecise_dtypes=True)
            nc.gpsimd.iota(step_no, [[1, STEPS]], base=0, channel_multiplier=0, allow_small_or_imprecise_dtypes=True)
            nc.gpsimd.iota(part_no, [[0, 1]], base=0, channel_multiplier=1, allow_small_or_imprecise_dtypes=True)
            nc.gpsimd.iota(node_no[:, :], [[1, P]], base=0, channel_multiplier=0, allow_small_or_imprecise_dtypes=True)
            nc.gpsimd.memset(ident[:, :], 0.0).then_inc(pads_set, 1)
            pool.wait_ge(pads_set, 2)
            nc.gpsimd.affine_select(out=ident[:, :], in_=ident[:, :], compare_op=ALU.not_equal, fill=1.0, base=0,
                                    pattern=[[-1, P]], channel_multiplier=1)
            last = mask[:, NT - 1:NT]
            nc.gpsimd.affine_select(out=last, in_=last, compare_op=ALU.is_gt, fill=0.0, base=TAIL,
                                    pattern=[[0, 1]], channel_multiplier=-1).then_inc(consts_set, 1)
            def gather(layer):
                with pool.Fori(0, GROUPS) as g:
                    for h in range(2):
                        pool.wait_ge(ring_free, (g + layer * GROUPS) * RING + (h + 1) * HALF)
                        nc.gpsimd.tensor_copy(idx_now[:, h * HALF:(h + 1) * HALF],
                                              idx[:, bass.ds(g * RING + h * HALF, HALF)]).then_inc(idx_copied, 1)
                        pool.wait_ge(idx_copied, (g + layer * GROUPS) * 2 + h + 1)
                        alone(pool)
                        for i in range(h * HALF, (h + 1) * HALF):
                            nc.gpsimd.indirect_dma_start(
                                ring[:, i, :], None, (msg1, msg2)[layer],
                                bass.IndirectOffsetOnAxis(ap=idx_now[:, i:i + 1], axis=0)).then_inc(slot_full[i], 16)

            for layer in range(2):
                for c in range(CH):
                    pool.wait_ge(part_sent[c], 16 * NT * (layer + 1))
                gather(layer)

        @block.scalar
        def _(act):
            n = 0
            act.wait_ge(consts_set, 1)
            for name, w in (("s", W_slice), ("q", W_q), ("k", W_k), ("v", W_v)):
                for h2 in range(2):
                    act.dma_start(bd[name][h2 * C:(h2 + 1) * C, h2 * C:(h2 + 1) * C], w).then_inc(ld_small, 16)
                    n += 1
            for t, a in ((b1_bo, b1), (b2_all, b2)):
                act.dma_start(t[:, :], a.rearrange("(a n) -> a n", a=1).to_broadcast([P, D])).then_inc(ld_small, 16)
                n += 1
            act.dma_start(bsl, b_slice.rearrange("(a n) -> a n", a=1).to_broadcast([P, G])).then_inc(ld_small, 16)
            act.dma_start(temp_all, temperature.rearrange("a h b c -> a (h b c)").to_broadcast([P, H])).then_inc(ld_small, 16)
            act.dma_start(bfx_col[:, :], b_fx.rearrange("(a p) -> p a", p=P)).then_inc(ld_small, 16)
            act.dma_start(bx_col[:, :], b_x.rearrange("(a p) -> p a", p=P)).then_inc(ld_small, 16)
            act.dma_start(wx, W_x.rearrange("(k p) m -> p k m", p=P)).then_inc(ld_small, 16)
            act.dma_start(wfx[:, :, :], W_fx.rearrange("(k p) m -> p k m", p=P)).then_inc(ld_small, 16)
            act.dma_start(wout[:, :, :], W_out.rearrange("(a p) m -> p a m", p=P)).then_inc(ld_small, 16)
            n += 7
            assert n == SMALL_LOADS
            for a in range(HP):
                act.wait_ge(wxT_mm, a + 1)
                if a:
                    act.wait_ge(wlog_mm, a)
                nc.scalar.copy(wxT, bank["tr"][:, 0:D]).then_inc(wxT_saved, 1)

            def save_xT(n, par):
                act.wait_ge(tr_done, n + 1)
                nc.scalar.copy(xT[:, par, :, :].rearrange("p k n -> p (k n)"), bank["tr"][:, 0:D]).then_inc(xT_ready, 1)

            def root(n):
                act.wait_ge(var_ready, n + 1)
                nc.scalar.activation(std[:, 0, :], mv[:, 0, 1:2], ACT.Sqrt, bias=eps[:, :], scale=1.0).then_inc(std_ready, 1)

            def hi(tile, c):
                act.wait_ge(chunk_mm, tile * CH + c + 1)
                nc.scalar.copy(parts[:, c, :, 0, :], chunk[c % 2][:, :].rearrange("p (r d) -> p r d", r=2)).then_inc(hi_ready, 1)

            def mid(tile, c):
                act.wait_ge(res_ready, tile * CH + c + 1 + 2)
                nc.scalar.copy(parts[:, c, :, 1, :], resid[:, c % 2, :].rearrange("p (r d) -> p r d", r=2)).then_inc(mid_ready, 1)

            def transform(j, par, more):
                if more:
                    root(j + 1)
                for c in range(CH):
                    act.wait_ge(part_sent[c], j * 16)
                    hi(j, c)
                    if c:
                        mid(j, c - 1)
                    if c == 2 and more:
                        save_xT(j + 1, 1 - par)
                mid(j, CH - 1)

            root(0)
            save_xT(0, 0)
            with act.Fori(0, NT // 2 - 1) as jj:
                for par in range(2):
                    transform(jj * 2 + par, par, True)
            transform(NT - 2, 0, True)
            transform(NT - 1, 1, False)
            act.dma_start(xin[:, 0, :], x[0:P, :]).then_inc(xin_full[0], 16)

            def hidden(j):
                save_xT(j + NT, 0)
                def send(c):
                    act.wait_ge(lo_ready, (j + NT) * CH + c + 1)
                    act.dma_start(msg_tiles[1][bass.ds(j, 1), :, c * 2 * ROW:(c + 1) * 2 * ROW].rearrange("a p d -> (a p) d"),
                                  parts[:, c, :, :, :].rearrange("p r h d -> p (r h d)")).then_inc(part_sent[c], 16)
                for c in range(CH + 2):
                    if c < CH:
                        act.wait_ge(part_sent[c], (j + NT) * 16)
                        hi(j + NT, c)
                    if 1 <= c <= CH:
                        mid(j + NT, c - 1)
                    if c >= 2:
                        send(c - 2)
                act.wait_ge(base_ready, j + 1)

            with act.Fori(0, NT - 2) as j:
                hidden(j)
                act.dma_start(xin[:, 0, :], x[bass.ds((j + 1) * P, P), :]).then_inc(xin_full[0], 16)
            hidden(NT - 2)
            act.dma_start(xin[0:TAIL, 0, :], x[N - TAIL:N, :]).then_inc(xin_full[0], 16)
            hidden(NT - 1)
            act.dma_start(b1_bo[:, :], b_out.rearrange("(a n) -> a n", a=1).to_broadcast([P, D])).then_inc(ld_bo, 16)
            act.sem_inc(swT_saved, 1)

            def save_swT(j):
                act.wait_ge(swT_done, j + 1)
                nc.scalar.copy(swT[:, :, bass.ds(j * P, P)], chunk[1][:, :].rearrange("p (a n) -> p a n", a=HP)).then_inc(swT_saved, 1)

            def behind(j):
                save_xT(j + 2 * NT, 0)
                nc.scalar.copy(xn[:, 1, :], xn[:, 0, :]).then_inc(prev_ready, 1)
                act.wait_ge(logit_ready, j + 1)
                nc.scalar.activation(logit[:, :], logit[:, :], ACT.Exp).then_inc(exp_ready, 1)

            root(NT)
            root(NT + 1)
            behind(0)
            with act.Fori(0, NT - 2) as j:
                root(j + NT + 2)
                save_swT(j)
                behind(j + 1)
            save_swT(NT - 2)
            behind(NT - 1)
            save_swT(NT - 1)
            act.wait_ge(qkv_mm, 1)
            for n3, name in enumerate(("agg0", "tr", "self")):
                nc.scalar.copy(qkvT[n3], bank[name][:, 0:HP * G].rearrange("p (a g) -> p a g", a=HP)).then_inc(qkv_saved, 1)
            act.wait_ge(score_ready, 1)
            nc.scalar.activation(att, att, ACT.Exp, scale=SCALE).then_inc(score_exp, 1)
            act.wait_ge(vo_mm, 1)
            for h2 in range(2):
                for half in range(2):
                    nc.scalar.copy(vo[0:G, 4 * half + h2:4 * half + h2 + 3:2, :],
                                   bank[VO_BANKS[2 * h2 + half]][0:G, :].rearrange("p (h d) -> p h d", h=2)).then_inc(vo_saved, 1)
            act.wait_ge(mix_mm, 1)
            for half, name in enumerate(MIX_BANKS):
                nc.scalar.copy(mix[:, 2 * half:2 * half + 2, :], bank[name][:, :].rearrange("p (a d) -> p a d", a=2)).then_inc(mix_saved, 1)
            with act.Fori(0, NT // 2) as jj:
                for par in range(2):
                    j = jj * 2 + par
                    act.wait_ge(out_mm, j + 1)
                    nc.scalar.copy(swTile[:, par, :, :], swT[:, :, bass.ds(j * P, P)]).then_inc(tile_copied, 1)

        @block.vector
        def _(dve):
            ch = Chain(dve, dve_prep)
            dve.wait_ge(ld_edges, 16 * EDGE_LOADS)
            dve.wait_ge(consts_set, 1)
            ch.done(nc.vector.tensor_scalar(out=lo_i, in0=dst_t[:, :, 0], scalar1=7, scalar2=None, op0=ALU.logical_shift_right))
            nc.vector.memset(lo_i[0:1, 0:1], 0)
            ch.done(nc.vector.tensor_scalar(out=hi_i, in0=nxt_t, scalar1=7, scalar2=None, op0=ALU.logical_shift_right))
            ch.done(nc.vector.tensor_tensor(out=start_lo, in0=lo_i, in1=tile_no, op=ALU.add))
            ch.done(nc.vector.scalar_tensor_tensor(out=start_hi, in0=hi_i, scalar=1.0, in1=tile_no, op0=ALU.add, op1=ALU.add))
            for c in range(EC):
                nc.vector.tensor_scalar(out=ge_lo[:, c, :], in0=step_no, scalar1=start_lo[:, c:c + 1], scalar2=None, op0=ALU.is_ge)
                ch.done(nc.vector.tensor_scalar(out=ge_hi[:, c, :], in0=step_no, scalar1=start_hi[:, c:c + 1], scalar2=None, op0=ALU.is_ge))
            nc.vector.tensor_tensor(out=ge_hi, in0=ge_lo, in1=ge_hi, op=ALU.subtract)
            nc.vector.scalar_tensor_tensor(out=row_f, in0=src_t, scalar=float(R), in1=rel_t, op0=ALU.mult, op1=ALU.add)
            nc.vector.tensor_copy(dst_f, dst_t).then_inc(edges_ready, 1)
            dve.wait_ge(step_mm, 1)
            ch.done(nc.vector.scalar_tensor_tensor(out=nt_of, in0=step_no, scalar=1.0, in1=bank["agg0"][:, 0:STEPS], op0=ALU.add, op1=ALU.subtract))
            nc.vector.tensor_copy(idx[:, :], bank["self"][:, 0:STEPS])
            nc.vector.scalar_tensor_tensor(out=seg[:, :], in0=nt_of, scalar=-float(P), in1=bank["c1"][:, 0:STEPS],
                                           op0=ALU.mult, op1=ALU.add)
            ch.done(nc.vector.tensor_scalar(out=le, in0=nt_of, scalar1=part_no, scalar2=None, op0=ALU.is_le))
            nc.vector.tensor_reduce(out=endc, in_=le, axis=AX.X, op=ALU.add).then_inc(endc_ready, 1)
            dve.wait_ge(ends_mm, 1)
            ch.done(nc.vector.tensor_scalar(out=ends[:, :], in0=bank["tr"][0:1, 0:P], scalar1=-1.0, scalar2=None, op0=ALU.add))
            nc.vector.memset(ends[0:1, NT:], 1 << 20).then_inc(ends_ready, 1)
            dve.wait_ge(ld_small, 16 * SMALL_LOADS)
            ch.done(nc.vector.tensor_scalar(out=itemp, in0=temp_all, scalar1=0.1, scalar2=5.0, op0=ALU.max, op1=ALU.min))
            ch.done(nc.vector.reciprocal(itemp, itemp))
            nc.vector.tensor_copy(bx_all, bx_col[:, :].rearrange("p (a n) -> p a n", n=1).to_broadcast([P, HP, P])).then_inc(bx_ready, 1)
            for a in range(HP):
                dve.wait_ge(wlog_mm, a + 1)
                pair = slice(a * P, (a + 1) * P)
                two = itemp[:, 2 * a:2 * a + 2].rearrange("p (h g) -> p h g", g=1).to_broadcast([P, 2, G])
                for k in range(K2):
                    nc.vector.tensor_tensor(out=heads(wlog[:, k, pair]), in0=heads(chunk[0][:, k * P:(k + 1) * P]), in1=two, op=ALU.mult)
                ch.done(nc.vector.tensor_tensor(out=heads(blog[:, pair]), in0=heads(chunk[0][:, 2 * P:3 * P]),
                                        in1=bsl.rearrange("p (a g) -> p a g", a=1).to_broadcast([P, 2, G]), op=ALU.add))
                nc.vector.tensor_tensor(out=heads(blog[:, pair]), in0=heads(blog[:, pair]), in1=two, op=ALU.mult).then_inc(wlog_saved, 1)
            nc.vector.sem_inc(res_ready, 2)
            nc.vector.sem_inc(self_free, 1)
            dve.wait_ge(wlog_saved, HP)

            def stats_of(n, rows):
                alone(dve)
                nc.vector.bn_stats(stats[:, :], rows).then_inc(norm1_steps, 1)
                dve.wait_ge(norm1_steps, n + 1)
                alone(dve)
                nc.vector.bn_aggr(mv[:, 0, :], stats[:, :]).then_inc(var_ready, 1)

            def normalize(n, rows, par):
                dve.wait_ge(std_ready, n + 1)
                nc.vector.reciprocal(rstd[:, 0, :], std[:, 0, :]).then_inc(norm2_steps, 1)
                dve.wait_ge(norm2_steps, n + 1)
                nc.vector.tensor_scalar(out=xn[:, par, :], in0=rows, scalar1=mv[:, 0, 0:1], scalar2=rstd[:, 0, :],
                                        op0=ALU.subtract, op1=ALU.mult).then_inc(xn_ready, 1)

            left = [resid[:, b, :].rearrange("p (r d) -> p r d", r=2) for b in range(2)]

            def rest(tile, c):
                if c != 1:
                    dve.wait_ge(lo_ready, tile * CH + max(c - 1, 0))
                dve.wait_ge(hi_ready, tile * CH + c + 1)
                nc.vector.tensor_tensor(out=left[c % 2], in0=chunk[c % 2][:, :].rearrange("p (r d) -> p r d", r=2),
                                        in1=parts[:, c, :, 0, :], op=ALU.subtract).then_inc(res_ready, 1)

            def low(tile, c):
                dve.wait_ge(mid_ready, tile * CH + c + 1)
                nc.vector.tensor_tensor(out=parts[:, c, :, 2, :], in0=left[c % 2], in1=parts[:, c, :, 1, :], op=ALU.subtract).then_inc(lo_ready, 1)

            def one_hots(g):
                nc.vector.tensor_tensor(
                    out=onehot[:, bass.ds(g * RING, RING), :],
                    in0=node_no[:, :].rearrange("p (a n) -> p a n", a=1).to_broadcast([P, RING, P]),
                    in1=seg[:, bass.ds(g * RING, RING)].rearrange("p (s a) -> p s a", a=1).to_broadcast([P, RING, P]),
                    op=ALU.is_equal).then_inc(onehot_ready, 1)

            def transform(j, jj, par, more):
                if more:
                    dve.wait_ge(xin_full[1 - par], (jj + 1 + par) * 16)
                    stats_of(j + 1, xin[:, 1 - par, :])
                dve.wait_ge(self_mm, j + 1)
                nc.vector.tensor_tensor(out=tile_at(base, j), in0=bank["self"][:, 0:D], in1=b1_bo[:, :], op=ALU.add).then_inc(self_free, 1)
                rest(j, 0)
                rest(j, 1)
                if more:
                    normalize(j + 1, xin[:, 1 - par, :], 1 - par)
                low(j, 0)
                rest(j, 2)
                low(j, 1)
                rest(j, 3)
                low(j, 2)
                low(j, 3)
                one_hots(j)

            dve.wait_ge(xin_full[0], 16)
            stats_of(0, xin[:, 0, :])
            normalize(0, xin[:, 0, :], 0)
            with dve.Fori(0, NT // 2 - 1) as jj:
                for par in range(2):
                    transform(jj * 2 + par, jj, par, True)
            transform(NT - 2, NT // 2 - 1, 0, True)
            transform(NT - 1, NT // 2 - 1, 1, False)
            for g in range(NT, GROUPS):
                one_hots(g)

            def hidden(j, par):
                dve.wait_ge(agg_done, j + 1)
                dve.wait_ge(tr_done, j + NT)
                nc.vector.tensor_tensor(out=xn[:, 0, :], in0=aggs[par], in1=tile_at(base, j), op=ALU.add).then_inc(agg_free, 1)
                dve.wait_ge(agg_free, j + 2)
                nc.vector.tensor_scalar(out=xn[:, 0, :], in0=xn[:, 0, :], scalar1=0.0, scalar2=None, op0=ALU.max).then_inc(xn_ready, 1)

            def messages(j):
                dve.wait_ge(self_mm, j + NT + 1)
                dve.wait_ge(xin_full[0], (j + NT // 2 + 1) * 16)
                nc.vector.tensor_tensor(out=tile_at(base, j), in0=bank["self"][:, 0:D], in1=xin[:, 0, :], op=ALU.add).then_inc(self_free, 1)
                dve.wait_ge(self_free, j + NT + 2)
                nc.vector.tensor_tensor(out=tile_at(base, j), in0=tile_at(base, j), in1=b2_all[:, :], op=ALU.add).then_inc(base_ready, 1)
                for c in range(CH + 1):
                    if c < CH:
                        rest(j + NT, c)
                    if c:
                        low(j + NT, c - 1)

            nc.vector.sem_inc(agg_free, 1)
            hidden(0, 0)
            with dve.Fori(0, NT // 2 - 1) as jj:
                for odd in range(2):
                    hidden(jj * 2 + odd + 1, 1 - odd)
                    messages(jj * 2 + odd)
            hidden(NT - 1, 1)
            messages(NT - 2)
            messages(NT - 1)

            def second(j, par):
                rows = tile_at(base, j)
                dve.wait_ge(agg_done, j + NT + 1)
                nc.vector.tensor_tensor(out=rows, in0=aggs[par], in1=rows, op=ALU.add).then_inc(agg_free, 1)
                dve.wait_ge(agg_free, j + NT + 2)
                stats_of(j + NT, rows)
                dve.wait_ge(prev_ready, j)
                normalize(j + NT, rows, 0)

            def weights(j):
                c = Chain(dve, slice_steps, j, 5)
                dve.wait_ge(logit_mm, j + 1)
                c.done(nc.vector.tensor_tensor(out=logit[:, :], in0=chunk[0][:, :], in1=blog[:, :], op=ALU.add))
                c.done(nc.vector.tensor_reduce(out=hmax[:, :], in_=heads(logit[:, :]), axis=AX.X, op=ALU.max))
                nc.vector.tensor_tensor(out=heads(logit[:, :]), in0=heads(logit[:, :]),
                                        in1=hmax[:, :].rearrange("p (h g) -> p h g", g=1).to_broadcast([P, H, G]),
                                        op=ALU.subtract).then_inc(logit_ready, 1)
                dve.wait_ge(exp_ready, j + 1)
                c.done(nc.vector.tensor_reduce(out=hsum[:, :], in_=heads(logit[:, :]), axis=AX.X, op=ALU.add))
                c.done(nc.vector.reciprocal(hsum[:, :], hsum[:, :]))
                c.done(nc.vector.tensor_scalar(out=hsum[:, :], in0=hsum[:, :], scalar1=mask[:, bass.ds(j, 1)], scalar2=None, op0=ALU.mult))
                nc.vector.tensor_tensor(out=heads(sw[:, :]), in0=heads(logit[:, :]),
                                        in1=hsum[:, :].rearrange("p (h g) -> p h g", g=1).to_broadcast([P, H, G]),
                                        op=ALU.mult).then_inc(sw_ready, 1)
                dve.wait_ge(sw_ready, j + 1)
                nc.vector.tensor_tensor(out=swsum[:, :], in0=swsum[:, :], in1=sw[:, :], op=ALU.add).then_inc(swsum_steps, 1)
                assert c.n == 5

            second(0, 0)
            with dve.Fori(0, NT // 2 - 1) as jj:
                for odd in range(2):
                    second(jj * 2 + odd + 1, 1 - odd)
                    weights(jj * 2 + odd)
            second(NT - 1, 1)
            weights(NT - 2)
            weights(NT - 1)

            ch = Chain(dve, tail_steps)
            dve.wait_ge(norm_mm, 1)
            nrm = bank["self"][:, :]
            ch.done(nc.vector.tensor_scalar(out=rnorm, in0=nrm, scalar1=EPS_SLICE, scalar2=None, op0=ALU.add))
            ch.done(nc.vector.reciprocal(rnorm, rnorm))
            for m in range(K2):
                nc.vector.tensor_tensor(out=ttn[:, m, :], in0=bank[f"t{m}"][:, :], in1=rnorm, op=ALU.mult).then_inc(ttn_ready, 1)
            ch.done(nc.vector.tensor_tensor(out=cnorm, in0=nrm, in1=rnorm, op=ALU.mult))
            for h2 in range(2):
                rows = slice(h2 * C, (h2 + 1) * C)
                ch.done(nc.vector.tensor_tensor(
                    out=tokC[rows, :, :], in0=cnorm[rows, :].rearrange("p (a n) -> p a n", a=HP)[:, :, h2 * G:(h2 + 1) * G],
                    in1=bfx_col[rows, :].rearrange("p (a n) -> p a n", n=1).to_broadcast([C, HP, G]), op=ALU.mult))
            dve.wait_ge(tok_mm, 1)
            for h2 in range(2):
                rows = slice(h2 * C, (h2 + 1) * C)
                nc.vector.tensor_tensor(
                    out=tokC[rows, :, :], in0=tokC[rows, :, :],
                    in1=bank["c0"][rows, :].rearrange("p (a n) -> p a n", a=HP)[:, :, h2 * G:(h2 + 1) * G],
                    op=ALU.add).then_inc(tok_ready, 1)
            dve.wait_ge(score_mm, 1)
            for h2 in range(2):
                rows = slice(h2 * G, (h2 + 1) * G)
                s3 = bank[f"t{h2}"][rows, 0:HP * G].rearrange("p (a g) -> p a g", a=HP)
                ch.done(nc.vector.tensor_reduce(out=amax[rows, :], in_=s3, axis=AX.X, op=ALU.max))
                ch.done(nc.vector.tensor_tensor(out=att[rows, :, :], in0=s3,
                                                in1=amax[rows, :].rearrange("p (a n) -> p a n", n=1).to_broadcast([G, HP, G]), op=ALU.subtract))
            nc.vector.sem_inc(score_ready, 1)
            dve.wait_ge(score_exp, 1)
            ch.done(nc.vector.tensor_reduce(out=asum, in_=att, axis=AX.X, op=ALU.add))
            ch.done(nc.vector.reciprocal(asum, asum))
            nc.vector.tensor_tensor(out=att, in0=att, in1=asum.rearrange("p (a n) -> p a n", n=1).to_broadcast([P, HP, G]),
                                    op=ALU.mult).then_inc(att_ready, 1)
            dve.wait_ge(attT_mm, 1)
            nc.vector.tensor_copy(attT[0:G, :, :], bank["agg1"][0:G, :].rearrange("p (a n) -> p a n", a=HP)).then_inc(attT_saved, 1)
            dve.wait_ge(ld_bo, 16)
            nc.vector.sem_inc(out_added, 2)
            with dve.Fori(0, NT // 2) as jj:
                for par in range(2):
                    j = jj * 2 + par
                    with dve.If(jj > 0):
                        dve.wait_ge(res_sent[par], jj * 16)
                        alone(dve)
                    dve.wait_ge(out_mm, 2 + j + 1)
                    nc.vector.tensor_tensor(out=res[:, par, :], in0=bank[f"c{par}"][:, 0:D], in1=tile_at(base, j), op=ALU.add).then_inc(out_added, 1)
                    dve.wait_ge(out_added, j + 3)
                    nc.vector.tensor_tensor(out=res[:, par, :], in0=res[:, par, :], in1=b1_bo[:, :], op=ALU.add).then_inc(out_ready, 1)

        @block.tensor
        def _(pe):
            mm = nc.tensor.matmul
            pe.wait_ge(consts_set, 1)
            pe.wait_ge(edges_ready, 1)
            for lhsT, rhs, to in ((None, ge_lo, "agg0"), (row_f, ge_hi, "self"), (dst_f, ge_hi, "c1")):
                for c in range(EC):
                    last = mm(bank[to][:, 0:STEPS], ones[:, :] if lhsT is None else lhsT[:, c, :], rhs[:, c, :],
                              start=(c == 0), stop=(c == EC - 1))
            last.then_inc(step_mm, 1)
            pe.wait_ge(endc_ready, 1)
            mm(bank["tr"][0:1, 0:P], endc, ident[:, :], start=True, stop=True).then_inc(ends_mm, 1)
            pe.wait_ge(ends_ready, 1)
            pe.wait_ge(bx_ready, 1)
            for a in range(HP):
                pair = slice(a * P, (a + 1) * P)
                if a:
                    pe.wait_ge(wxT_saved, a)
                for k in range(K2):
                    last = nc.tensor.transpose(bank["tr"][:, k * P:(k + 1) * P], wx[:, k, pair], ident[:, :])
                last.then_inc(wxT_mm, 1)
                pe.wait_ge(wxT_saved, a + 1)
                if a:
                    pe.wait_ge(wlog_saved, a)
                for k in range(K2):
                    mm(chunk[0][:, k * P:(k + 1) * P], wxT[:, k * P:(k + 1) * P], bd["s"][:, :], start=True, stop=True)
                mm(chunk[0][:, 2 * P:3 * P], bx_all[:, a, :], bd["s"][:, :], start=True, stop=True).then_inc(wlog_mm, 1)

            def transposes(n, par):
                pe.wait_ge(xn_ready, n + 1)
                for k in range(K2):
                    last = nc.tensor.transpose(bank["tr"][:, k * P:(k + 1) * P], xn[:, par, k * P:(k + 1) * P], ident[:, :])
                last.then_inc(tr_done, 1)

            def products(tile, par, chunks):
                if 0 in chunks:
                    pe.wait_ge(xT_ready, tile + 1)
                    pe.wait_ge(self_free, tile + 1)
                    for k in range(K2):
                        last = mm(bank["self"][:, 0:D], xT[:, par, k, :], wself[:, k, :], start=(k == 0), stop=(k == K2 - 1))
                    last.then_inc(self_mm, 1)
                for c in chunks:
                    pe.wait_ge(res_ready, tile * CH + c + 1)
                    for k in range(K2):
                        last = mm(chunk[c % 2][:, :], xT[:, par, k, :], wrel[:, k, c * CW:(c + 1) * CW], start=(k == 0), stop=(k == K2 - 1))
                    last.then_inc(chunk_mm, 1)

            pe.wait_ge(wlog_saved, HP)
            pe.wait_ge(ld_w1, 16 * (K2 + 1))
            transposes(0, 0)
            with pe.Fori(0, NT // 2 - 1) as jj:
                for par in range(2):
                    j = jj * 2 + par
                    products(j, par, (0, 1, 2))
                    transposes(j + 1, 1 - par)
                    products(j, par, (3,))
            products(NT - 2, 0, (0, 1, 2))
            transposes(NT - 1, 1)
            products(NT - 2, 0, (3,))
            products(NT - 1, 1, range(CH))

            def zero(out, start):
                return mm(out, zeros[:, 0:P], zeros[:, :], start=start, stop=True, skip_group_check=True)

            def hidden(t):
                transposes(t + NT, 0)
                products(t + NT, 0, range(CH))

            def logits(t):
                transposes(t + 2 * NT, 0)
                pe.wait_ge(xT_ready, t + 2 * NT + 1)
                for k in range(K2):
                    last = mm(chunk[0][:, :], xT[:, 0, k, :], wlog[:, k, :], start=(k == 0), stop=(k == K2 - 1))
                last.then_inc(logit_mm, 1)

            def slices(t):
                pe.wait_ge(sw_ready, t + 1)
                for m in range(K2):
                    mm(bank[f"t{m}"][:, :], xn[:, 1, m * P:(m + 1) * P], sw[:, :], start=False, stop=True, skip_group_check=True)
                pe.wait_ge(swT_saved, t + 1)
                for a in range(HP):
                    last = nc.tensor.transpose(chunk[1][:, a * P:(a + 1) * P], sw[:, a * P:(a + 1) * P], ident[:, :])
                last.then_inc(swT_done, 1)

            tile = pe.alloc_register("tile")
            behind = pe.alloc_register("behind")
            sliced = pe.alloc_register("sliced")
            turn = pe.alloc_register("turn")
            end = pe.alloc_register("end")
            node_tile = lambda reg: pe.snap(reg, min_val=0, max_val=NT - 1)
            sum_at = lambda: agg2[:, bass.ds(pe.snap(turn, min_val=0, max_val=512), D)]
            pe.sem_inc(ring_free, RING)
            pe.wait_ge(onehot_ready, GROUPS)
            zero(aggs[0], True)
            pe.reg_mov(turn, 0)
            for layer in range(2):
                for reg in (tile, behind, sliced):
                    pe.reg_mov(reg, 0)
                pe.reg_mov(end, pe.value_load(ends[0:1, 0:1]))
                if layer:
                    pe.wait_ge(self_free, 2 * NT + 1)
                    for m in range(K2):
                        mm(bank[f"t{m}"][:, :], zeros[:, 0:P], onehot[:, 0:4, :].rearrange("p s n -> p (s n)"),
                           start=True, stop=True, skip_group_check=True)
                with pe.Fori(0, GROUPS) as g:
                    for i in range(RING):
                        s = g * RING + i
                        out_sum = sum_at()
                        pe.wait_ge(rows_ready, s + layer * STEPS + 1)
                        for part in range(3):
                            last = mm(out_sum, onehot[:, bass.ds(s, 1), :].rearrange("p a n -> p (a n)"),
                                      ring[:, i, part * D:(part + 1) * D],
                                      start=False, stop=True, skip_group_check=True)
                        last.then_inc(ring_free, 1)
                        with pe.If(pe.snap(end) == s):
                            zero(out_sum, False).then_inc(agg_done, 1)
                            pe.reg_alu(turn, turn, 512, ALU.bitwise_xor)
                            pe.wait_ge(agg_free, node_tile(tile) + layer * NT + 1)
                            zero(sum_at(), True)
                            with pe.If(pe.snap(tile) > 0):
                                if layer:
                                    with pe.If(pe.snap(behind) > 0):
                                        slices(node_tile(sliced))
                                        pe.reg_add(sliced, sliced, 1)
                                    logits(node_tile(behind))
                                else:
                                    pe.wait_ge(ld_w2, 16 * (K2 + 1))
                                    hidden(node_tile(behind))
                                pe.reg_add(behind, behind, 1)
                            pe.reg_add(tile, tile, 1)
                            pe.reg_mov(end, pe.value_load(ends[0:1, bass.ds(pe.snap(tile, min_val=0, max_val=NT), 1)]))
                if layer:
                    slices(NT - 2)
                    logits(NT - 1)
                    slices(NT - 1)
                else:
                    hidden(NT - 1)

            pe.wait_ge(swsum_steps, NT)
            mm(bank["self"][:, :], ones[:, :], swsum[:, :], start=True, stop=True).then_inc(norm_mm, 1)
            pe.wait_ge(ttn_ready, K2)
            for a in range(HP):
                pair = slice(a * P, (a + 1) * P)
                for k in range(K2):
                    last = mm(bank["c0"][:, pair], wfx[:, k, pair], ttn[:, k, pair], start=(k == 0), stop=(k == K2 - 1))
            last.then_inc(tok_mm, 1)
            pe.wait_ge(tok_ready, 2)
            tok = tokC.rearrange("p a g -> p (a g)")
            for name, to in (("q", "agg0"), ("k", "tr"), ("v", "self")):
                last = mm(bank[to][:, 0:HP * G], bd[name][:, :], tok, start=True, stop=True)
            last.then_inc(qkv_mm, 1)
            pe.wait_ge(qkv_saved, 3)
            qT, kT, vT = qkvT
            for h2 in range(2):
                rows = slice(h2 * G, (h2 + 1) * G)
                for a in range(HP):
                    last = mm(bank[f"t{h2}"][rows, a * G:(a + 1) * G], qT[rows, a, :], kT[rows, a, :], start=True, stop=True)
            last.then_inc(score_mm, 1)
            for h2 in range(2):
                rows = slice(h2 * G, (h2 + 1) * G)
                for a in range(HP):
                    last = mm(bank[VO_BANKS[2 * h2 + a // 2]][0:G, (a % 2) * D:(a % 2 + 1) * D], vT[rows, a, :], wout[rows, a, :], start=True, stop=True)
            last.then_inc(vo_mm, 1)
            pe.wait_ge(att_ready, 1)
            for a in range(HP):
                last = nc.tensor.transpose(bank["agg1"][0:G, a * P:(a + 1) * P], att[:, a, :], ident[:, :])
            last.then_inc(attT_mm, 1)
            pe.wait_ge(attT_saved, 1)
            pe.wait_ge(vo_saved, 4)
            for h2 in range(2):
                rows = slice(h2 * G, (h2 + 1) * G)
                for a in range(HP):
                    last = mm(bank[MIX_BANKS[a // 2]][rows, (a % 2) * D:(a % 2 + 1) * D], attT[0:G, a, rows], vo[0:G, 2 * a + h2, :], start=True, stop=True)
            last.then_inc(mix_mm, 1)
            pe.wait_ge(mix_saved, 2)
            pe.sem_inc(out_mm, 2)
            with pe.Fori(0, NT // 2) as jj:
                for par in range(2):
                    j = jj * 2 + par
                    pe.wait_ge(tile_copied, j + 1)
                    pe.wait_ge(out_added, j + 1)
                    for a in range(HP):
                        last = mm(bank[f"c{par}"][:, 0:D], swTile[:, par, a, :], mix[:, a, :], start=(a == 0), stop=(a == HP - 1))
                    last.then_inc(out_mm, 1)


_INS = ['x', 'src', 'dst', 'edge_type_8', 'L0_gnn_W1', 'L0_gnn_self_w1', 'L0_gnn_b1', 'L0_gnn_W2', 'L0_gnn_self_w2', 'L0_gnn_b2',
        'L0_ffn_W_fx', 'L0_ffn_b_fx', 'L0_ffn_W_x', 'L0_ffn_b_x', 'L0_ffn_W_slice', 'L0_ffn_b_slice', 'L0_ffn_W_q', 'L0_ffn_W_k',
        'L0_ffn_W_v', 'L0_ffn_W_out', 'L0_ffn_b_out', 'L0_ffn_temperature']


def kernel(**inputs):
    import concourse.bacc as bacc
    from concourse.bass_utils import run_bass_kernel_spmd

    nc = bacc.Bacc("TRN2", target_bir_lowering=False, num_devices=1)
    arrays, args = {}, []
    for name in _INS:
        a = np.ascontiguousarray(inputs[name])
        arrays[f"in_{name}"] = a
        args.append(nc.dram_tensor(f"in_{name}", a.shape, mybir.dt.from_np(a.dtype), kind="ExternalInput").ap())
    out = nc.dram_tensor("out", (N, D), f32, kind="ExternalOutput").ap()
    rgcn_slice_attention(nc, *args, out)
    r = run_bass_kernel_spmd(nc, [arrays], core_ids=[0])
    return r.results[0]["out"]
```

```python
import concourse.bass as bass
from concourse import mybir
from contextlib import ExitStack
import numpy as np

f32 = mybir.dt.float32
bf16 = mybir.dt.bfloat16
i32 = mybir.dt.int32
u32 = mybir.dt.uint32
ALU = mybir.AluOpType
ACT = mybir.ActivationFunctionType
AX = mybir.AxisListType

P = 128
N, E, D, R = 2500, 40000, 256, 8
K2 = D // P
NT = -(-N // P)
TAIL = N - (NT - 1) * P
ET = -(-E // P)
EC = -(-ET // P)
RING = 20
BATCH = 4
QUAD = 4
STEPS = -(-(ET + NT - 1) // RING) * RING
GROUPS = STEPS // RING
SHARE = STEPS // NT
CUTS = (0, 4, 10, SHARE)
assert SHARE * NT == STEPS and SHARE > CUTS[2]
USED = -(-(ET + NT - 1) // QUAD) * QUAD
LAST = USED - (GROUPS - 1) * RING
assert LAST % BATCH == 0 and RING % BATCH == 0 and RING % QUAD == 0
ROW = 3 * D
CH = 4
CW = R * D // CH
H, C, G = 8, 64, 64
HP = H // 2
HG = H * G
EPS_LN = 1e-5
EPS_SLICE = 1e-5
SCALE = float(C) ** -0.5
ER = max(r for r in range(1, P + 1) if E % r == 0)
EW = E // ER
NO_NODE = 4096


class Chain:

    def __init__(self, eng, sem, it=0, per_turn=0):
        self.eng, self.sem, self.base, self.n = eng, sem, it * per_turn, 0

    def done(self, ins):
        self.n += 1
        ins.then_inc(self.sem, 1)
        self.eng.wait_ge(self.sem, self.base + self.n)


def rgcn_slice_attention(nc, x, src, dst, rel, W1, self_w1, b1, W2, self_w2, b2, W_fx, b_fx, W_x, b_x,
                         W_slice, b_slice, W_q, W_k, W_v, W_out, b_out, temperature, out):
    msg1 = nc.dram_tensor("msg1", (NT * P * R, ROW), bf16, kind="Internal").ap()
    msg2 = nc.dram_tensor("msg2", (NT * P * R, ROW), bf16, kind="Internal").ap()
    by_tile = nc.dram_tensor("by_tile", (E, 3), i32, kind="Internal").ap()
    msg_tiles = [m.rearrange("(t p r) d -> t p (r d)", p=P, r=R) for m in (msg1, msg2)]

    with ExitStack() as ctx:
        ctx.enter_context(nc.allow_non_contiguous_dma(reason="a few small columns of biases and indices"))
        sb = lambda name, shape, dt=f32: ctx.enter_context(nc.sbuf_tensor(name, shape, dt))
        sem = lambda name: ctx.enter_context(nc.semaphore(name))

        onehot = sb("onehot", [P, STEPS, P], bf16)
        ring = sb("ring", [P, RING, ROW], bf16)
        base = sb("base", [P, NT, D])
        area = sb("area", [P, HP * NT * P])
        wrel = area[:, 0:K2 * R * D].rearrange("p (k m) -> p k m", k=K2)
        o = K2 * R * D
        parts = area[:, o:o + CH * 2 * ROW // 2].bitcast(bf16).rearrange("p (c r h d) -> p c r h d", c=CH, r=2, h=3)
        o += CH * 2 * ROW // 2
        resid = area[:, o:o + 2 * CW].rearrange("p (b m) -> p b m", b=2)
        swT = area[:, :].rearrange("p (a n) -> p a n", a=HP)
        idx = sb("idx", [P, STEPS], i32)
        idx_now = sb("idx_now", [P, 2, RING], u32)
        seg = sb("seg", [P, STEPS])
        wself = sb("wself", [P, K2, D])
        wlog = sb("wlog", [P, K2, HG])
        b1_bo = sb("b1_bo", [P, D])
        b2_all = sb("b2_all", [P, D])
        blog = sb("blog", [P, HG])
        xin = sb("xin", [P, 2, D])
        xn = sb("xn", [P, 2, D])
        xT = sb("xT", [P, 2, K2, P])
        logit = sb("logit", [P, HG])
        sw = sb("sw", [P, HG])
        swsum = sb("swsum", [P, HG])
        ident = sb("ident", [P, P])
        ones = sb("ones", [P, P])
        zeros = sb("zeros", [P, D], bf16)
        bd = {n: sb(f"bd_{n}", [P, P]) for n in ("s", "q", "k", "v")}
        bfx_col = sb("bfx_col", [P, HP])
        bx_col = sb("bx_col", [P, HP])
        ends = sb("ends", [1, P], i32)
        unsorted = sb("unsorted", [1, 1], i32)
        eps = sb("eps", [P, 1])
        mask = sb("mask", [P, NT])
        stats = sb("stats", [P, 6])
        mv = sb("mv", [P, 2, 2])
        std = sb("std", [P, 2, 1])
        rstd = sb("rstd", [P, 2, 1])
        hmax = sb("hmax", [P, H])
        hsum = sb("hsum", [P, H])

        ringf = ring[:, :, :].rearrange("p s d -> p (s d)").bitcast(f32)
        ringi = ring[:, :, :].rearrange("p s d -> p (s d)").bitcast(i32)
        at = [0]

        def cut(view, *dims):
            n = int(np.prod(dims))
            got = view[:, at[0]:at[0] + n]
            at[0] += n
            return got.rearrange("p (a b) -> p a b", a=dims[0]) if len(dims) == 2 else got

        src_t, dst_t, rel_t = (cut(ringi, EC, P) for _ in range(3))
        nxt_t, lo_i, hi_i = (cut(ringi, EC) for _ in range(3))
        tile_no = cut(ringf, EC)
        start_lo, start_hi = cut(ringf, EC), cut(ringf, EC)
        key_i, nxt_key = cut(ringi, EC, P), cut(ringi, EC)
        drops = cut(ringf, EC, P)
        drop_n = cut(ringf, 1)
        row_f, dst_f = cut(ringf, EC, P), cut(ringf, EC, P)
        ge_lo, ge_hi = cut(ringf, EC, STEPS), cut(ringf, EC, STEPS)
        step_no = cut(ringf, STEPS)
        nt_of = cut(ringf, STEPS)
        endc = cut(ringf, 1)
        part_no = cut(ringf, 1)
        assert at[0] <= RING * ROW // 2
        ohf = onehot[:, :, :].rearrange("p s n -> p (s n)").bitcast(f32)
        wx = ohf[:, 0:K2 * HG].rearrange("p (k m) -> p k m", k=K2)
        wxT = ohf[:, 1024:1024 + K2 * HG].rearrange("p (k m) -> p k m", k=K2)
        bx_all = ohf[:, 2048:2048 + P * HP].rearrange("p (a n) -> p a n", a=HP)
        temp_all = ohf[:, 2560:2560 + H]
        itemp = ohf[:, 2576:2576 + H]
        bsl = ohf[:, 2592:2592 + G]
        le = ohf[:, 2816:2816 + STEPS]
        ohi = onehot[:, :, :].rearrange("p s n -> p (s n)").bitcast(i32)
        at[0] = 0
        in_tile, rank, rank2 = (cut(ohf, NT * EW).rearrange("p (b t) -> p b t", b=NT) for _ in range(3))
        edge = cut(ohi, EW, 3)
        edge_now = cut(ohi, RING, 3)
        tile_of = cut(ohi, EW)
        pos = cut(ohf, EW)
        pos_now = cut(ohi, RING).bitcast(u32)
        before = cut(ohf, P)
        total = cut(ohf, P)
        first = cut(ohf, NT)
        assert at[0] <= STEPS * P // 2
        node_no = sb("node_no", [P, P], bf16)
        at[0] = 0
        ttn = cut(ringf, K2, HG)
        rnorm, cnorm = cut(ringf, HP, G), cut(ringf, HP, G)
        tokC = cut(ringf, HP, G)
        qkvT = [cut(ringf, HP, G) for _ in range(3)]
        att = cut(ringf, HP, G)
        attT = cut(ringf, HP, P)
        vo = cut(ringf, H, D)
        amax, asum = cut(ringf, HP), cut(ringf, HP)
        assert at[0] <= RING * ROW // 2
        wfx = onehot[:, 48:64, :].rearrange("p s n -> p (s n)").bitcast(f32).rearrange("p (k m) -> p k m", k=K2)
        wout = onehot[:, 64:80, :].rearrange("p s n -> p (s n)").bitcast(f32).rearrange("p (a m) -> p a m", a=HP)
        mix = onehot[:, 0:16, :].rearrange("p s n -> p (s n)").bitcast(f32).rearrange("p (a d) -> p a d", a=HP)
        swTile = onehot[:, 16:32, :].rearrange("p s n -> p (s n)").bitcast(f32).rearrange("p (b a n) -> p b a n", b=2, a=HP)
        res = onehot[:, 32:48, :].rearrange("p s n -> p (s n)").bitcast(f32)[:, 0:2 * D].rearrange("p (b d) -> p b d", b=2)

        bank = {n: ctx.enter_context(nc.psum_tensor(n, [P, 512], f32))
                for n in ("tr", "self", "c0", "c1", "t0", "t1")}
        agg2 = ctx.enter_context(nc.psum_tensor("agg2", [P, 2 * 512], f32))
        bank["agg0"], bank["agg1"] = agg2[:, 0:512], agg2[:, 512:1024]
        aggs, chunk = [agg2[:, 0:D], agg2[:, 512:512 + D]], [bank["c0"], bank["c1"]]

        xin_full = [sem("xin_full0"), sem("xin_full1")]
        part_sent = [sem(f"part_sent{c}") for c in range(CH)]
        slot_full = [sem(f"slot_full{i}") for i in range(RING)]
        res_sent = [sem("res_sent0"), sem("res_sent1")]
        names = """pads_set consts_set bd_set ld_edges ld_slice ld_small ld_w1 ld_w2 ld_tail ld_bo dve_prep edges_ready step_mm
        ends_mm ends_ready bx_ready wxT_mm wxT_saved wlog_mm wlog_saved onehot_ready tables_ready
        sort_loaded sort_steps totals_ready total_mm total_ready first_mm pos_ready edge_copied edge_moved
        sort_reloaded edges2_ready step2_mm endc2_ready ends2_mm
        var_ready std_ready xn_ready tr_done xT_ready self_free self_mm chunk_mm hi_ready res_ready mid_ready lo_ready
        idx_copied ring_free agg_done agg_free base_ready
        logit_mm logit_ready exp_ready sw_ready swT_done swT_saved
        norm1_steps norm2_steps prev_ready slice_steps swsum_steps tail_steps
        sums_done norm_mm ttn_ready tok_mm tok_ready qkv_mm qkv_saved score_mm score_ready score_exp att_ready attT_mm attT_saved
        vo_mm vo_saved mix_mm mix_saved tile_copied out_mm out_added out_ready""".split()
        sems = {name: sem(name) for name in names}
        (pads_set, consts_set, bd_set, ld_edges, ld_slice, ld_small, ld_w1, ld_w2, ld_tail, ld_bo, dve_prep, edges_ready, step_mm,
         ends_mm, ends_ready, bx_ready, wxT_mm, wxT_saved, wlog_mm, wlog_saved, onehot_ready, tables_ready,
         sort_loaded, sort_steps, totals_ready, total_mm, total_ready, first_mm, pos_ready, edge_copied, edge_moved,
         sort_reloaded, edges2_ready, step2_mm, endc2_ready, ends2_mm,
         var_ready, std_ready, xn_ready, tr_done, xT_ready, self_free, self_mm, chunk_mm, hi_ready, res_ready, mid_ready, lo_ready,
         idx_copied, ring_free, agg_done, agg_free, base_ready,
         logit_mm, logit_ready, exp_ready, sw_ready, swT_done, swT_saved,
         norm1_steps, norm2_steps, prev_ready, slice_steps, swsum_steps, tail_steps,
         sums_done, norm_mm, ttn_ready, tok_mm, tok_ready, qkv_mm, qkv_saved, score_mm, score_ready, score_exp, att_ready, attT_mm, attT_saved,
         vo_mm, vo_saved, mix_mm, mix_saved, tile_copied, out_mm, out_added, out_ready) = (sems[name] for name in names)

        VO_BANKS, MIX_BANKS = ("agg0", "tr", "self", "c1"), ("t0", "t1")

        past = {e.engine: sem(f"past_{n}") for n, e in (("pool", nc.gpsimd), ("act", nc.scalar), ("dve", nc.vector))}

        def alone(eng):
            eng.sem_inc(past[eng.engine], 1)

        def tile_at(view, j):
            return view[:, bass.ds(j, 1), :].rearrange("p a n -> p (a n)")

        def heads(view):
            return view.rearrange("p (h g) -> p h g", g=G)

        block = ctx.enter_context(nc.Block())

        EDGE_LOADS, EDGE2_LOADS, SLICE_LOADS, SMALL_LOADS = 3 * 3 + EC, 3 * (EC + 1) + EC, 6, 9

        @block.sync
        def _(sp):
            for par in range(2):
                sp.dma_start(xin[:, par, :], x[par * P:(par + 1) * P, :]).then_inc(xin_full[par], 16)

            def load_edges(arrays, chunks, loaded):
                whole = (E // P) * P
                full = (E // (P * P)) * P * P
                for arr, t in zip(arrays, (dst_t, src_t, rel_t)):
                    for c in range(0, EC - 1, chunks):
                        sp.dma_start(t[:, c:c + chunks, :], arr[c * P * P:(c + chunks) * P * P].rearrange("(c t e) -> t c e", e=P, t=P)).then_inc(loaded, 16)
                    sp.dma_start(t[0:(whole - full) // P, EC - 1, :], arr[full:whole].rearrange("(t e) -> t e", e=P)).then_inc(loaded, 16)
                    r0 = (whole - full) // P
                    sp.dma_start(t[r0:r0 + 1, EC - 1, 0:E - whole], arr[whole:E].rearrange("(t e) -> t e", t=1)).then_inc(loaded, 16)
                firsts = arrays[0][P:E:P].rearrange("(t e) -> t e", e=1)
                for c in range(EC):
                    m = min(P, ET - 1 - c * P)
                    sp.dma_start(nxt_t[0:m, c:c + 1], firsts[c * P:c * P + m, :]).then_inc(loaded, 16)

            sp.wait_ge(pads_set, 1)
            load_edges((dst, src, rel), EC - 1, ld_edges)
            n = 0
            for t, a in ((b1_bo, b1), (b2_all, b2)):
                sp.dma_start(t[:, :], a.rearrange("(a n) -> a n", a=1).to_broadcast([P, D])).then_inc(ld_small, 16)
                n += 1
            for name, w in (("q", W_q), ("k", W_k), ("v", W_v)):
                for h2 in range(2):
                    sp.dma_start(bd[name][h2 * C:(h2 + 1) * C, h2 * C:(h2 + 1) * C], w).then_inc(ld_small, 16)
                    n += 1
            sp.dma_start(bfx_col[:, :], b_fx.rearrange("(a p) -> p a", p=P)).then_inc(ld_small, 16)
            n += 1
            assert n == SMALL_LOADS

            def send_table(jj, full):
                for par in range(2):
                    j = jj * 2 + par
                    if full:
                        sp.wait_ge(xn_ready, j + 1)
                    if par < full:
                        sp.dma_start(xin[:, par, :], x[bass.ds((j + 2) * P, P), :]).then_inc(xin_full[par], 16)
                    elif full:
                        sp.dma_start(xin[0:TAIL, par, :], x[N - TAIL:N, :]).then_inc(xin_full[par], 16)
                    for c in range(CH):
                        sp.wait_ge(lo_ready, j * CH + c + 2)
                        sp.dma_start(msg_tiles[0][bass.ds(j, 1), :, c * 2 * ROW:(c + 1) * 2 * ROW].rearrange("a p d -> (a p) d"),
                                     parts[:, c, :, :, :].rearrange("p r h d -> p (r h d)")).then_inc(part_sent[c], 16)

            with sp.Fori(0, NT // 2 - 2) as jj:
                send_table(jj, 2)
            send_table(NT // 2 - 2, 1)
            send_table(NT // 2 - 1, 0)
            sp.wait_ge(ends_ready, 1)
            with sp.If(sp.value_load(unsorted[0:1, 0:1]) > 0):
                sp.wait_ge(onehot_ready, 3 * NT)
                for n3, arr in enumerate((src, dst, rel)):
                    sp.dma_start(edge[0:ER, :, n3:n3 + 1], arr.rearrange("(p t a) -> p t a", p=ER, a=1)).then_inc(sort_loaded, 16)
                sp.wait_ge(edge_moved, 16 * EW)
                column = by_tile.rearrange("e c -> c e")
                load_edges((column[1], column[0], column[2]), 1, sort_reloaded)
                sp.wait_ge(sort_reloaded, 16 * EDGE2_LOADS)
            sp.wait_ge(chunk_mm, NT * CH)
            for k in range(K2):
                sp.dma_start(wrel[:, k, :].rearrange("p (r m) -> p r m", r=R), W2[:, k * P:(k + 1) * P, :].rearrange("r p m -> p r m")).then_inc(ld_w2, 16)
            sp.dma_start(wself[:, :, :], self_w2.rearrange("(k p) m -> p k m", p=P)).then_inc(ld_w2, 16)
            for par in range(2):
                sp.dma_start(xin[:, par, :], x[par * P:(par + 1) * P, :]).then_inc(xin_full[par], 16)

            def send_hidden_table(jj, full):
                for par in range(2):
                    j = jj * 2 + par
                    for c in range(CH):
                        sp.wait_ge(lo_ready, (j + NT) * CH + c + 2)
                        sp.dma_start(msg_tiles[1][bass.ds(j, 1), :, c * 2 * ROW:(c + 1) * 2 * ROW].rearrange("a p d -> (a p) d"),
                                     parts[:, c, :, :, :].rearrange("p r h d -> p (r h d)")).then_inc(part_sent[c], 16)
                        if c == 0 and full:
                            sp.wait_ge(base_ready, j + 1)
                            if par < full:
                                sp.dma_start(xin[:, par, :], x[bass.ds((j + 2) * P, P), :]).then_inc(xin_full[par], 16)
                            else:
                                sp.dma_start(xin[0:TAIL, par, :], x[N - TAIL:N, :]).then_inc(xin_full[par], 16)

            with sp.Fori(0, NT // 2 - 2) as jj:
                send_hidden_table(jj, 2)
            send_hidden_table(NT // 2 - 2, 1)
            send_hidden_table(NT // 2 - 1, 0)
            sp.wait_ge(ring_free, RING + 2 * USED)
            sp.dma_start(wfx, W_fx.rearrange("(k p) m -> p k m", p=P)).then_inc(ld_tail, 16)
            sp.dma_start(wout, W_out.rearrange("(a p) m -> p a m", p=P)).then_inc(ld_tail, 16)
            with sp.Fori(0, NT // 2 - 1) as jj:
                for par in range(2):
                    sp.wait_ge(out_ready, jj * 2 + par + 1)
                    sp.dma_start(out[bass.ds((jj * 2 + par) * P, P), :], res[:, par, :]).then_inc(res_sent[par], 16)
            sp.wait_ge(out_ready, NT - 1)
            sp.dma_start(out[(NT - 2) * P:(NT - 1) * P, :], res[:, 0, :]).then_inc(res_sent[0], 16)
            sp.wait_ge(out_ready, NT)
            sp.dma_start(out[N - TAIL:N, :], res[0:TAIL, 1, :]).then_inc(res_sent[1], 16)
            for par in range(2):
                sp.wait_ge(res_sent[par], 16 * (NT // 2 + 1))

        @block.gpsimd
        def _(pool):
            for m in bd.values():
                last = nc.gpsimd.memset(m[:, :], 0.0)
            last.then_inc(bd_set, 1)
            nc.gpsimd.memset(dst_t, NO_NODE)
            nc.gpsimd.memset(src_t, 0)
            nc.gpsimd.memset(rel_t, 0)
            nc.gpsimd.memset(nxt_t, NO_NODE).then_inc(pads_set, 1)
            nc.gpsimd.memset(ones[:, :], 1.0)
            nc.gpsimd.memset(zeros[:, :], 0.0)
            nc.gpsimd.memset(swsum[:, :], 0.0)
            nc.gpsimd.memset(eps[:, :], EPS_LN)
            nc.gpsimd.memset(mask[:, :], 1.0)
            nc.gpsimd.iota(tile_no, [[P, EC]], base=0, channel_multiplier=1, allow_small_or_imprecise_dtypes=True)
            nc.gpsimd.iota(step_no, [[1, STEPS]], base=0, channel_multiplier=0, allow_small_or_imprecise_dtypes=True)
            nc.gpsimd.iota(part_no, [[0, 1]], base=0, channel_multiplier=1, allow_small_or_imprecise_dtypes=True)
            nc.gpsimd.iota(node_no[:, :], [[1, P]], base=0, channel_multiplier=0, allow_small_or_imprecise_dtypes=True)
            nc.gpsimd.memset(ident[:, :], 0.0).then_inc(pads_set, 1)
            pool.wait_ge(pads_set, 2)
            nc.gpsimd.affine_select(out=ident[:, :], in_=ident[:, :], compare_op=ALU.not_equal, fill=1.0, base=0,
                                    pattern=[[-1, P]], channel_multiplier=1)
            last = mask[:, NT - 1:NT]
            nc.gpsimd.affine_select(out=last, in_=last, compare_op=ALU.is_gt, fill=0.0, base=TAIL,
                                    pattern=[[0, 1]], channel_multiplier=-1).then_inc(consts_set, 1)

            def gather_ring(layer, g, buf, slots, more):
                pool.wait_ge(idx_copied, g + layer * GROUPS + 1)
                for first in range(0, slots, BATCH):
                    pool.wait_ge(ring_free, layer * USED + g * RING + first + BATCH)
                    if more and first + BATCH == slots:
                        nc.gpsimd.tensor_copy(idx_now[:, 1 - buf, :], idx[:, bass.ds((g + 1) * RING, RING)]).then_inc(idx_copied, 1)
                    elif not isinstance(g, int):
                        alone(pool)
                    for i in range(first, first + BATCH):
                        nc.gpsimd.indirect_dma_start(
                            ring[:, i, :], None, (msg1, msg2)[layer],
                            bass.IndirectOffsetOnAxis(ap=idx_now[:, buf, i:i + 1], axis=0)).then_inc(slot_full[i], 16)

            def gather(layer):
                pool.wait_ge(ring_free, RING + layer * USED)
                nc.gpsimd.tensor_copy(idx_now[:, 0, :], idx[:, 0:RING]).then_inc(idx_copied, 1)
                with pool.Fori(0, (GROUPS - 1) // 2) as gg:
                    for buf in range(2):
                        gather_ring(layer, gg * 2 + buf, buf, RING, True)
                for g in range((GROUPS - 1) // 2 * 2, GROUPS):
                    gather_ring(layer, g, g % 2, RING if g < GROUPS - 1 else LAST, g < GROUPS - 1)

            pool.sem_inc(lo_ready, 1)
            with pool.Fori(0, NT) as j:
                for c in range(CH):
                    pool.wait_ge(mid_ready, j * CH + c + 1)
                    nc.gpsimd.tensor_tensor(out=parts[:, c, :, 2, :], in0=resid[:, c % 2, :].rearrange("p (r d) -> p r d", r=2),
                                            in1=parts[:, c, :, 1, :], op=ALU.subtract).then_inc(lo_ready, 1)
            pool.wait_ge(ends_ready, 1)
            with pool.If(pool.value_load(unsorted[0:1, 0:1]) > 0):
                pool.wait_ge(sort_loaded, 16 * 3)
                pool.wait_ge(pos_ready, 1)

                def move(b):
                    nc.gpsimd.tensor_copy(pos_now[0:ER, :], pos[0:ER, bass.ds(b * RING, RING)]).then_inc(edge_copied, 1)
                    nc.gpsimd.tensor_copy(edge_now[0:ER, :, :], edge[0:ER, bass.ds(b * RING, RING), :]).then_inc(edge_copied, 1)
                    pool.wait_ge(edge_copied, (b + 1) * 2)
                    alone(pool)
                    for i in range(RING):
                        nc.gpsimd.indirect_dma_start(by_tile, bass.IndirectOffsetOnAxis(ap=pos_now[0:ER, i:i + 1], axis=0),
                                                     edge_now[0:ER, i, :], None).then_inc(edge_moved, 16)

                move(0)
                with pool.Fori(1, EW // RING) as b:
                    pool.wait_ge(edge_moved, b * RING * 16)
                    move(b)
            pool.wait_ge(tables_ready, 1)
            for layer in range(2):
                for c in range(CH):
                    pool.wait_ge(part_sent[c], 16 * (NT * (layer + 1) + 1))
                gather(layer)

        @block.scalar
        def _(act):
            act.dma_start(wx, W_x.rearrange("(k p) m -> p k m", p=P)).then_inc(ld_slice, 16)
            act.dma_start(bx_col[:, :], b_x.rearrange("(a p) -> p a", p=P)).then_inc(ld_slice, 16)
            act.dma_start(bsl, b_slice.rearrange("(a n) -> a n", a=1).to_broadcast([P, G])).then_inc(ld_slice, 16)
            act.dma_start(temp_all, temperature.rearrange("a h b c -> a (h b c)").to_broadcast([P, H])).then_inc(ld_slice, 16)
            act.wait_ge(bd_set, 1)
            for h2 in range(2):
                act.dma_start(bd["s"][h2 * C:(h2 + 1) * C, h2 * C:(h2 + 1) * C], W_slice).then_inc(ld_slice, 16)
            for k in range(K2):
                act.dma_start(wrel[:, k, :].rearrange("p (r m) -> p r m", r=R), W1[:, k * P:(k + 1) * P, :].rearrange("r p m -> p r m")).then_inc(ld_w1, 16)
            act.dma_start(wself[:, :, :], self_w1.rearrange("(k p) m -> p k m", p=P)).then_inc(ld_w1, 16)

            def save_xT(n, par):
                act.wait_ge(tr_done, n + 1)
                nc.scalar.copy(xT[:, par, :, :].rearrange("p k n -> p (k n)"), bank["tr"][:, 0:D]).then_inc(xT_ready, 1)

            def root(n):
                act.wait_ge(var_ready, n + 1)
                nc.scalar.activation(std[:, 0, :], mv[:, 0, 1:2], ACT.Sqrt, bias=eps[:, :], scale=1.0).then_inc(std_ready, 1)

            def hi(tile, c):
                act.wait_ge(chunk_mm, tile * CH + c + 1)
                nc.scalar.copy(parts[:, c, :, 0, :], chunk[c % 2][:, :].rearrange("p (r d) -> p r d", r=2)).then_inc(hi_ready, 1)

            def mid(tile, c):
                act.wait_ge(res_ready, tile * CH + c + 1 + 2)
                nc.scalar.copy(parts[:, c, :, 1, :], resid[:, c % 2, :].rearrange("p (r d) -> p r d", r=2)).then_inc(mid_ready, 1)

            def transform(j, par, more):
                if more:
                    root(j + 1)
                for c in range(CH):
                    act.wait_ge(part_sent[c], (j + 1) * 16)
                    hi(j, c)
                    if c == 2 and more:
                        save_xT(j + 1, 1 - par)
                    mid(j, c)

            for c in range(CH):
                act.sem_inc(part_sent[c], 16)
            root(0)
            act.wait_ge(wxT_mm, 1)
            for k in range(K2):
                nc.scalar.copy(wxT[:, k, :], bank[f"t{k}"][:, :]).then_inc(wxT_saved, 1)
            save_xT(0, 0)
            with act.Fori(0, NT // 2 - 1) as jj:
                for par in range(2):
                    transform(jj * 2 + par, par, True)
            transform(NT - 2, 0, True)
            transform(NT - 1, 1, False)
            with act.Fori(0, NT) as j:
                save_xT(j + NT, 0)
                for c in range(CH + 1):
                    if c < CH:
                        act.wait_ge(part_sent[c], (j + NT + 1) * 16)
                        hi(j + NT, c)
                    if c:
                        mid(j + NT, c - 1)
            act.dma_start(b1_bo[:, :], b_out.rearrange("(a n) -> a n", a=1).to_broadcast([P, D])).then_inc(ld_bo, 16)
            act.sem_inc(swT_saved, 1)

            def save_swT(j):
                act.wait_ge(swT_done, j + 1)
                nc.scalar.copy(swT[:, :, bass.ds(j * P, P)], chunk[1][:, :].rearrange("p (a n) -> p a n", a=HP)).then_inc(swT_saved, 1)

            def behind(j, between=lambda: None):
                save_xT(j + 2 * NT, 0)
                between()
                nc.scalar.copy(xn[:, 1, :], xn[:, 0, :]).then_inc(prev_ready, 1)
                act.wait_ge(logit_ready, j + 1)
                nc.scalar.activation(logit[:, :], logit[:, :], ACT.Exp).then_inc(exp_ready, 1)

            root(NT)
            root(NT + 1)
            behind(0)
            with act.Fori(0, NT - 2) as j:
                root(j + NT + 2)
                behind(j + 1, lambda: save_swT(j))
            behind(NT - 1, lambda: save_swT(NT - 2))
            save_swT(NT - 1)
            act.wait_ge(sums_done, 1)
            for m in range(K2):
                nc.scalar.copy(ttn[:, m, :], bank[f"t{m}"][:, :]).then_inc(ttn_ready, 1)
            act.wait_ge(qkv_mm, 1)
            for n3, name in enumerate(("agg0", "tr", "self")):
                nc.scalar.copy(qkvT[n3], bank[name][:, 0:HP * G].rearrange("p (a g) -> p a g", a=HP)).then_inc(qkv_saved, 1)
            act.wait_ge(score_ready, 1)
            nc.scalar.activation(att, att, ACT.Exp, scale=SCALE).then_inc(score_exp, 1)
            act.wait_ge(vo_mm, 1)
            for h2 in range(2):
                for half in range(2):
                    nc.scalar.copy(vo[0:G, 4 * half + h2:4 * half + h2 + 3:2, :],
                                   bank[VO_BANKS[2 * h2 + half]][0:G, :].rearrange("p (h d) -> p h d", h=2)).then_inc(vo_saved, 1)
            act.wait_ge(mix_mm, 1)
            for half, name in enumerate(MIX_BANKS):
                nc.scalar.copy(mix[:, 2 * half:2 * half + 2, :], bank[name][:, :].rearrange("p (a d) -> p a d", a=2)).then_inc(mix_saved, 1)
            with act.Fori(0, NT // 2) as jj:
                for par in range(2):
                    j = jj * 2 + par
                    act.wait_ge(out_mm, j + 1)
                    nc.scalar.copy(swTile[:, par, :, :], swT[:, :, bass.ds(j * P, P)]).then_inc(tile_copied, 1)

        @block.vector
        def _(dve):
            ch = Chain(dve, dve_prep)
            dve.wait_ge(consts_set, 1)

            def step_starts(ch, ready):
                ch.done(nc.vector.tensor_scalar(out=lo_i, in0=dst_t[:, :, 0], scalar1=7, scalar2=None, op0=ALU.logical_shift_right))
                nc.vector.memset(lo_i[0:1, 0:1], 0)
                ch.done(nc.vector.tensor_scalar(out=hi_i, in0=nxt_t, scalar1=7, scalar2=None, op0=ALU.logical_shift_right))
                ch.done(nc.vector.tensor_tensor(out=start_lo, in0=lo_i, in1=tile_no, op=ALU.add))
                ch.done(nc.vector.scalar_tensor_tensor(out=start_hi, in0=hi_i, scalar=1.0, in1=tile_no, op0=ALU.add, op1=ALU.add))
                for c in range(EC):
                    nc.vector.tensor_scalar(out=ge_lo[:, c, :], in0=step_no, scalar1=start_lo[:, c:c + 1], scalar2=None, op0=ALU.is_ge)
                    ch.done(nc.vector.tensor_scalar(out=ge_hi[:, c, :], in0=step_no, scalar1=start_hi[:, c:c + 1], scalar2=None, op0=ALU.is_ge))
                nc.vector.tensor_tensor(out=ge_hi, in0=ge_lo, in1=ge_hi, op=ALU.subtract)
                nc.vector.scalar_tensor_tensor(out=row_f, in0=src_t, scalar=float(R), in1=rel_t, op0=ALU.mult, op1=ALU.add)
                nc.vector.tensor_copy(dst_f, dst_t).then_inc(ready, 1)

            def step_tables(ch, steps_mm):
                dve.wait_ge(steps_mm, 1)
                ch.done(nc.vector.scalar_tensor_tensor(out=nt_of, in0=step_no, scalar=1.0, in1=bank["agg0"][:, 0:STEPS], op0=ALU.add, op1=ALU.subtract))
                ch.done(nc.vector.scalar_tensor_tensor(out=seg[:, :], in0=nt_of, scalar=-float(P), in1=bank["t0"][:, 0:STEPS],
                                                       op0=ALU.mult, op1=ALU.add))
                ch.done(nc.vector.tensor_copy(idx[:, 0:STEPS], bank["agg1"][:, 0:STEPS]))
                ch.done(nc.vector.tensor_scalar(out=le, in0=nt_of, scalar1=part_no, scalar2=None, op0=ALU.is_le))
                return nc.vector.tensor_reduce(out=endc, in_=le, axis=AX.X, op=ALU.add)

            def tile_ends(ch):
                ch.done(nc.vector.tensor_scalar(out=ends[:, :], in0=bank["t1"][0:1, 0:P], scalar1=-1.0, scalar2=None, op0=ALU.add))
                ch.done(nc.vector.memset(ends[0:1, NT:], 1 << 20))

            dve.wait_ge(ld_slice, 16 * SLICE_LOADS)
            ch.done(nc.vector.tensor_scalar(out=itemp, in0=temp_all, scalar1=0.1, scalar2=5.0, op0=ALU.max, op1=ALU.min))
            ch.done(nc.vector.reciprocal(itemp, itemp))
            nc.vector.tensor_copy(bx_all, bx_col[:, :].rearrange("p (a n) -> p a n", n=1).to_broadcast([P, HP, P])).then_inc(bx_ready, 1)

            def stats_of(n, rows):
                alone(dve)
                nc.vector.bn_stats(stats[:, :], rows).then_inc(norm1_steps, 1)
                dve.wait_ge(norm1_steps, n + 1)
                alone(dve)
                nc.vector.bn_aggr(mv[:, 0, :], stats[:, :]).then_inc(var_ready, 1)

            def normalize(n, rows, par):
                dve.wait_ge(std_ready, n + 1)
                nc.vector.reciprocal(rstd[:, 0, :], std[:, 0, :]).then_inc(norm2_steps, 1)
                dve.wait_ge(norm2_steps, n + 1)
                nc.vector.tensor_scalar(out=xn[:, par, :], in0=rows, scalar1=mv[:, 0, 0:1], scalar2=rstd[:, 0, :],
                                        op0=ALU.subtract, op1=ALU.mult).then_inc(xn_ready, 1)

            left = [resid[:, b, :].rearrange("p (r d) -> p r d", r=2) for b in range(2)]

            def rest(tile, c):
                if c != 1:
                    dve.wait_ge(lo_ready, tile * CH + max(c - 1, 0) + 1)
                dve.wait_ge(hi_ready, tile * CH + c + 1)
                nc.vector.tensor_tensor(out=left[c % 2], in0=chunk[c % 2][:, :].rearrange("p (r d) -> p r d", r=2),
                                        in1=parts[:, c, :, 0, :], op=ALU.subtract).then_inc(res_ready, 1)

            def low(tile, c):
                dve.wait_ge(mid_ready, tile * CH + c + 1)
                nc.vector.tensor_tensor(out=parts[:, c, :, 2, :], in0=left[c % 2], in1=parts[:, c, :, 1, :], op=ALU.subtract).then_inc(lo_ready, 1)

            def one_hots(first, n):
                nc.vector.tensor_tensor(
                    out=onehot[:, bass.ds(first, n), :],
                    in0=node_no[:, :].rearrange("p (a n) -> p a n", a=1).to_broadcast([P, n, P]),
                    in1=seg[:, bass.ds(first, n)].rearrange("p (s a) -> p s a", a=1).to_broadcast([P, n, P]),
                    op=ALU.is_equal).then_inc(onehot_ready, 1)

            def transform(j, jj, par, more):
                dve.wait_ge(self_mm, j + 1)
                nc.vector.tensor_tensor(out=tile_at(base, j), in0=bank["self"][:, 0:D], in1=b1_bo[:, :], op=ALU.add).then_inc(self_free, 1)
                if more:
                    dve.wait_ge(xin_full[1 - par], (jj + 1 + par) * 16)
                    stats_of(j + 1, xin[:, 1 - par, :])
                one_hots(j * SHARE, CUTS[1])
                rest(j, 0)
                if more:
                    normalize(j + 1, xin[:, 1 - par, :], 1 - par)
                one_hots(j * SHARE + CUTS[1], CUTS[2] - CUTS[1])
                rest(j, 1)
                one_hots(j * SHARE + CUTS[2], CUTS[3] - CUTS[2])
                rest(j, 2)
                rest(j, 3)

            dve.wait_ge(xin_full[0], 16)
            stats_of(0, xin[:, 0, :])
            normalize(0, xin[:, 0, :], 0)
            dve.wait_ge(ld_edges, 16 * EDGE_LOADS)
            step_starts(ch, edges_ready)
            dve.wait_ge(wlog_mm, 1)
            per_head = itemp.rearrange("p (h g) -> p h g", g=1).to_broadcast([P, H, G])
            for k in range(K2):
                nc.vector.tensor_tensor(out=heads(wlog[:, k, :]), in0=heads(chunk[k][:, :]), in1=per_head, op=ALU.mult)
            ch.done(nc.vector.tensor_tensor(out=heads(blog[:, :]), in0=heads(bank["self"][:, :]),
                                            in1=bsl.rearrange("p (a g) -> p a g", a=1).to_broadcast([P, H, G]), op=ALU.add))
            nc.vector.tensor_tensor(out=heads(blog[:, :]), in0=heads(blog[:, :]), in1=per_head, op=ALU.mult).then_inc(wlog_saved, 1)
            dve.wait_ge(wlog_saved, 1)
            nc.vector.sem_inc(res_ready, 2)
            nc.vector.sem_inc(self_free, 1)
            ch.done(nc.vector.tensor_scalar(out=key_i, in0=dst_t, scalar1=7, scalar2=None, op0=ALU.logical_shift_right))
            ch.done(nc.vector.tensor_scalar(out=nxt_key, in0=nxt_t, scalar1=7, scalar2=None, op0=ALU.logical_shift_right))
            ch.done(nc.vector.tensor_tensor(out=drops[:, :, 0:P - 1], in0=key_i[:, :, 0:P - 1], in1=key_i[:, :, 1:P], op=ALU.is_gt))
            ch.done(nc.vector.tensor_tensor(out=drops[:, :, P - 1], in0=key_i[:, :, P - 1], in1=nxt_key, op=ALU.is_gt))
            ch.done(nc.vector.tensor_reduce(out=drop_n, in_=drops.rearrange("p c e -> p (c e)"), axis=AX.X, op=ALU.add))
            ch.done(step_tables(ch, step_mm))
            dve.wait_ge(ld_small, 16 * SMALL_LOADS)
            with dve.Fori(0, NT // 2 - 1) as jj:
                for par in range(2):
                    transform(jj * 2 + par, jj, par, True)
            transform(NT - 2, NT // 2 - 1, 0, True)
            transform(NT - 1, NT // 2 - 1, 1, False)
            dve.wait_ge(ends_mm, 1)
            tile_ends(ch)
            nc.vector.tensor_copy(unsorted[:, :], bank["t1"][0:1, P:P + 1]).then_inc(ends_ready, 1)
            dve.wait_ge(ends_ready, 1)
            with dve.If(dve.value_load(unsorted[0:1, 0:1]) > 0):
                cs = Chain(dve, sort_steps)
                dve.wait_ge(sort_loaded, 16 * 3)
                rows = slice(0, ER)
                cs.done(nc.vector.tensor_scalar(out=tile_of[rows, :], in0=edge[rows, :, 1], scalar1=7, scalar2=None, op0=ALU.logical_shift_right))
                spread = lambda v: v.rearrange("p (b t) -> p b t", t=1).to_broadcast([ER, NT, EW])
                cs.done(nc.vector.tensor_tensor(out=in_tile[rows], in0=tile_of[rows, :].rearrange("p (b t) -> p b t", b=1).to_broadcast([ER, NT, EW]),
                                                in1=spread(step_no[rows, 0:NT]), op=ALU.is_equal))
                cs.done(nc.vector.tensor_copy(rank[rows], in_tile[rows]))
                now, then, d = rank, rank2, 1
                while d < EW:
                    cs.done(nc.vector.tensor_copy(then[rows, :, 0:d], now[rows, :, 0:d]))
                    cs.done(nc.vector.tensor_tensor(out=then[rows, :, d:EW], in0=now[rows, :, d:EW], in1=now[rows, :, 0:EW - d], op=ALU.add))
                    now, then, d = then, now, 2 * d
                cs.done(nc.vector.tensor_scalar(out=before[:, :], in0=node_no[:, :], scalar1=part_no, scalar2=None, op0=ALU.is_gt))
                nc.vector.tensor_copy(then[rows, :, 0], now[rows, :, EW - 1]).then_inc(totals_ready, 1)
                dve.wait_ge(total_mm, 1)
                nc.vector.tensor_copy(total[0:NT, :], bank["t1"][0:NT, 0:P]).then_inc(total_ready, 1)
                dve.wait_ge(first_mm, 1)
                cs.done(nc.vector.tensor_scalar(out=first[rows, :], in0=bank["t0"][rows, 0:NT], scalar1=-1.0, scalar2=None, op0=ALU.add))
                cs.done(nc.vector.tensor_tensor(out=then[rows], in0=now[rows], in1=spread(first[rows, :]), op=ALU.add))
                cs.done(nc.vector.tensor_tensor(out=now[rows], in0=then[rows], in1=in_tile[rows], op=ALU.mult))
                nc.vector.tensor_reduce(out=pos[rows, :], in_=now[rows].rearrange("p b t -> p t b"), axis=AX.X, op=ALU.add).then_inc(pos_ready, 1)
                dve.wait_ge(sort_reloaded, 16 * EDGE2_LOADS)
                step_starts(cs, edges2_ready)
                step_tables(cs, step2_mm).then_inc(endc2_ready, 1)
                dve.wait_ge(ends2_mm, 1)
                tile_ends(cs)
                with dve.Fori(0, NT) as j:
                    one_hots(j * SHARE, SHARE)
                dve.wait_ge(onehot_ready, 4 * NT)
            nc.vector.sem_inc(tables_ready, 2)

            def hidden(j, par):
                dve.wait_ge(agg_done, j + 1)
                dve.wait_ge(tr_done, j + NT)
                nc.vector.tensor_tensor(out=xn[:, 0, :], in0=aggs[par], in1=tile_at(base, j), op=ALU.add).then_inc(agg_free, 1)
                dve.wait_ge(agg_free, j + 2)
                nc.vector.tensor_scalar(out=xn[:, 0, :], in0=xn[:, 0, :], scalar1=0.0, scalar2=None, op0=ALU.max).then_inc(xn_ready, 1)

            def messages(jj, par):
                j = jj * 2 + par
                dve.wait_ge(self_mm, j + NT + 1)
                dve.wait_ge(xin_full[par], (jj + NT // 2 + 1) * 16)
                nc.vector.tensor_tensor(out=tile_at(base, j), in0=bank["self"][:, 0:D], in1=xin[:, par, :], op=ALU.add).then_inc(self_free, 1)
                dve.wait_ge(self_free, j + NT + 2)
                nc.vector.tensor_tensor(out=tile_at(base, j), in0=tile_at(base, j), in1=b2_all[:, :], op=ALU.add).then_inc(base_ready, 1)
                for c in range(CH + 1):
                    if c < CH:
                        rest(j + NT, c)
                    if c:
                        low(j + NT, c - 1)

            nc.vector.sem_inc(agg_free, 1)
            hidden(0, 0)
            with dve.Fori(0, NT // 2 - 1) as jj:
                for odd in range(2):
                    hidden(jj * 2 + odd + 1, 1 - odd)
                    messages(jj, odd)
            hidden(NT - 1, 1)
            messages(NT // 2 - 1, 0)
            messages(NT // 2 - 1, 1)

            def second(j, par):
                rows = tile_at(base, j)
                dve.wait_ge(agg_done, j + NT + 1)
                nc.vector.tensor_tensor(out=rows, in0=aggs[par], in1=rows, op=ALU.add).then_inc(agg_free, 1)
                dve.wait_ge(agg_free, j + NT + 2)
                stats_of(j + NT, rows)
                if not (isinstance(j, int) and j == 0):
                    dve.wait_ge(prev_ready, j)
                normalize(j + NT, rows, 0)

            def weights(j):
                c = Chain(dve, slice_steps, j, 5)
                dve.wait_ge(logit_mm, j + 1)
                c.done(nc.vector.tensor_tensor(out=logit[:, :], in0=chunk[0][:, :], in1=blog[:, :], op=ALU.add))
                c.done(nc.vector.tensor_reduce(out=hmax[:, :], in_=heads(logit[:, :]), axis=AX.X, op=ALU.max))
                nc.vector.tensor_tensor(out=heads(logit[:, :]), in0=heads(logit[:, :]),
                                        in1=hmax[:, :].rearrange("p (h g) -> p h g", g=1).to_broadcast([P, H, G]),
                                        op=ALU.subtract).then_inc(logit_ready, 1)
                dve.wait_ge(exp_ready, j + 1)
                c.done(nc.vector.tensor_reduce(out=hsum[:, :], in_=heads(logit[:, :]), axis=AX.X, op=ALU.add))
                c.done(nc.vector.reciprocal(hsum[:, :], hsum[:, :]))
                c.done(nc.vector.tensor_scalar(out=hsum[:, :], in0=hsum[:, :], scalar1=mask[:, bass.ds(j, 1)], scalar2=None, op0=ALU.mult))
                nc.vector.tensor_tensor(out=heads(sw[:, :]), in0=heads(logit[:, :]),
                                        in1=hsum[:, :].rearrange("p (h g) -> p h g", g=1).to_broadcast([P, H, G]),
                                        op=ALU.mult).then_inc(sw_ready, 1)
                dve.wait_ge(sw_ready, j + 1)
                nc.vector.tensor_tensor(out=swsum[:, :], in0=swsum[:, :], in1=sw[:, :], op=ALU.add).then_inc(swsum_steps, 1)
                assert c.n == 5

            second(0, 0)
            with dve.Fori(0, NT // 2 - 1) as jj:
                for odd in range(2):
                    second(jj * 2 + odd + 1, 1 - odd)
                    weights(jj * 2 + odd)
            second(NT - 1, 1)
            weights(NT - 2)
            weights(NT - 1)

            ch = Chain(dve, tail_steps)
            dve.wait_ge(norm_mm, 1)
            halves = [(slice(h2 * C, (h2 + 1) * C), h2) for h2 in range(2)]
            own = lambda b, rows, h2: b[rows, :].rearrange("p (a n) -> p a n", a=HP)[:, :, h2 * G:(h2 + 1) * G]
            for rows, h2 in halves:
                ch.done(nc.vector.tensor_scalar(out=rnorm[rows], in0=own(bank["self"], rows, h2), scalar1=EPS_SLICE, scalar2=None, op0=ALU.add))
                ch.done(nc.vector.tensor_tensor(
                    out=cnorm[rows], in0=own(bank["self"], rows, h2),
                    in1=bfx_col[rows, :].rearrange("p (a n) -> p a n", n=1).to_broadcast([C, HP, G]), op=ALU.mult))
            ch.done(nc.vector.reciprocal(rnorm, rnorm))
            dve.wait_ge(tok_mm, 1)
            for rows, h2 in halves:
                ch.done(nc.vector.tensor_tensor(out=tokC[rows], in0=own(bank["c0"], rows, h2), in1=cnorm[rows], op=ALU.add))
            nc.vector.tensor_tensor(out=tokC, in0=tokC, in1=rnorm, op=ALU.mult).then_inc(tok_ready, 1)
            dve.wait_ge(score_mm, 1)
            for h2 in range(2):
                rows = slice(h2 * G, (h2 + 1) * G)
                s3 = bank[f"t{h2}"][rows, 0:HP * G].rearrange("p (a g) -> p a g", a=HP)
                ch.done(nc.vector.tensor_reduce(out=amax[rows, :], in_=s3, axis=AX.X, op=ALU.max))
                ch.done(nc.vector.tensor_tensor(out=att[rows, :, :], in0=s3,
                                                in1=amax[rows, :].rearrange("p (a n) -> p a n", n=1).to_broadcast([G, HP, G]), op=ALU.subtract))
            nc.vector.sem_inc(score_ready, 1)
            dve.wait_ge(score_exp, 1)
            ch.done(nc.vector.tensor_reduce(out=asum, in_=att, axis=AX.X, op=ALU.add))
            ch.done(nc.vector.reciprocal(asum, asum))
            nc.vector.tensor_tensor(out=att, in0=att, in1=asum.rearrange("p (a n) -> p a n", n=1).to_broadcast([P, HP, G]),
                                    op=ALU.mult).then_inc(att_ready, 1)
            dve.wait_ge(attT_mm, 1)
            nc.vector.tensor_copy(attT[0:G, :, :], bank["agg1"][0:G, :].rearrange("p (a n) -> p a n", a=HP)).then_inc(attT_saved, 1)
            dve.wait_ge(ld_bo, 16)
            nc.vector.sem_inc(out_added, 2)
            for par in range(2):
                nc.vector.sem_inc(res_sent[par], 16)
            with dve.Fori(0, NT // 2) as jj:
                for par in range(2):
                    j = jj * 2 + par
                    dve.wait_ge(res_sent[par], (jj + 1) * 16)
                    dve.wait_ge(out_mm, 2 + j + 1)
                    nc.vector.tensor_tensor(out=res[:, par, :], in0=bank[f"c{par}"][:, 0:D], in1=tile_at(base, j), op=ALU.add).then_inc(out_added, 1)
                    dve.wait_ge(out_added, j + 3)
                    nc.vector.tensor_tensor(out=res[:, par, :], in0=res[:, par, :], in1=b1_bo[:, :], op=ALU.add).then_inc(out_ready, 1)

        @block.tensor
        def _(pe):
            mm = nc.tensor.matmul
            pe.wait_ge(consts_set, 1)
            pe.wait_ge(ld_slice, 16 * SLICE_LOADS)
            for k in range(K2):
                for a in range(HP):
                    last = nc.tensor.transpose(bank[f"t{k}"][:, a * P:(a + 1) * P], wx[:, k, a * P:(a + 1) * P], ident[:, :])
            last.then_inc(wxT_mm, 1)

            def steps(ready):
                pe.wait_ge(ready, 1)
                for lhsT, rhs, to in ((None, ge_lo, "agg0"), (row_f, ge_hi, "agg1"), (dst_f, ge_hi, "t0")):
                    for c in range(EC):
                        last = mm(bank[to][:, 0:STEPS], ones[:, :] if lhsT is None else lhsT[:, c, :], rhs[:, c, :],
                                  start=(c == 0), stop=(c == EC - 1))
                return last

            def ends_row():
                return mm(bank["t1"][0:1, 0:P], endc, ident[:, :], start=True, stop=True)

            def transposes(n, par):
                pe.wait_ge(xn_ready, n + 1)
                for k in range(K2):
                    last = nc.tensor.transpose(bank["tr"][:, k * P:(k + 1) * P], xn[:, par, k * P:(k + 1) * P], ident[:, :])
                last.then_inc(tr_done, 1)

            def products(tile, par, chunks):
                if 0 in chunks:
                    pe.wait_ge(xT_ready, tile + 1)
                    pe.wait_ge(self_free, tile + 1)
                    for k in range(K2):
                        last = mm(bank["self"][:, 0:D], xT[:, par, k, :], wself[:, k, :], start=(k == 0), stop=(k == K2 - 1))
                    last.then_inc(self_mm, 1)
                for c in chunks:
                    pe.wait_ge(res_ready, tile * CH + c + 1)
                    for k in range(K2):
                        last = mm(chunk[c % 2][:, :], xT[:, par, k, :], wrel[:, k, c * CW:(c + 1) * CW], start=(k == 0), stop=(k == K2 - 1))
                    last.then_inc(chunk_mm, 1)

            transposes(0, 0)
            pe.wait_ge(wxT_saved, K2)
            pe.wait_ge(bx_ready, 1)
            for a in range(HP):
                pair = slice(a * P, (a + 1) * P)
                for k in range(K2):
                    mm(chunk[k][:, pair], wxT[:, k, pair], bd["s"][:, :], start=True, stop=True)
                last = mm(bank["self"][:, pair], bx_all[:, a, :], bd["s"][:, :], start=True, stop=True)
            last.then_inc(wlog_mm, 1)
            steps(edges_ready).then_inc(step_mm, 1)
            pe.wait_ge(ld_w1, 16 * (K2 + 1))
            with pe.Fori(0, NT // 2 - 1) as jj:
                for par in range(2):
                    j = jj * 2 + par
                    products(j, par, (0, 1, 2))
                    transposes(j + 1, 1 - par)
                    products(j, par, (3,))
            products(NT - 2, 0, (0, 1, 2))
            transposes(NT - 1, 1)
            products(NT - 2, 0, (3,))
            products(NT - 1, 1, range(CH))
            ends_row()
            mm(bank["t1"][0:1, P:P + 1], drop_n, ones[:, 0:1], start=True, stop=True).then_inc(ends_mm, 1)
            pe.wait_ge(ends_ready, 1)
            with pe.If(pe.value_load(unsorted[0:1, 0:1]) > 0):
                pe.wait_ge(totals_ready, 1)
                row_total = (rank2, rank)[(EW - 1).bit_length() % 2][0:ER, :, 0]
                mm(bank["t1"][0:NT, 0:P], row_total, ones[0:ER, :], start=True, stop=True).then_inc(total_mm, 1)
                pe.wait_ge(total_ready, 1)
                mm(bank["t0"][0:ER, 0:NT], before[0:ER, 0:ER], row_total, start=True, stop=False)
                mm(bank["t0"][0:ER, 0:NT], total[0:NT, 0:ER], before[0:NT, 0:NT], start=False, stop=True).then_inc(first_mm, 1)
                steps(edges2_ready).then_inc(step2_mm, 1)
                pe.wait_ge(endc2_ready, 1)
                ends_row().then_inc(ends2_mm, 1)
            pe.wait_ge(tables_ready, 1)

            def zero(out, start):
                return mm(out, zeros[:, 0:P], zeros[:, :], start=start, stop=True, skip_group_check=True)

            def logits(t):
                pe.wait_ge(xT_ready, t + 2 * NT + 1)
                for k in range(K2):
                    last = mm(chunk[0][:, :], xT[:, 0, k, :], wlog[:, k, :], start=(k == 0), stop=(k == K2 - 1))
                last.then_inc(logit_mm, 1)

            def slices(t):
                pe.wait_ge(sw_ready, t + 1)
                for m in range(K2):
                    mm(bank[f"t{m}"][:, :], xn[:, 1, m * P:(m + 1) * P], sw[:, :], start=False, stop=True, skip_group_check=True)
                pe.wait_ge(swT_saved, t + 1)
                for a in range(HP):
                    last = nc.tensor.transpose(chunk[1][:, a * P:(a + 1) * P], sw[:, a * P:(a + 1) * P], ident[:, :])
                last.then_inc(swT_done, 1)

            tile = pe.alloc_register("tile")
            behind = pe.alloc_register("behind")
            sliced = pe.alloc_register("sliced")
            turn = pe.alloc_register("turn")
            end = pe.alloc_register("end")
            node_tile = lambda reg: pe.snap(reg, min_val=0, max_val=NT - 1)
            sum_at = lambda: agg2[:, bass.ds(pe.snap(turn, min_val=0, max_val=512), D)]
            pe.sem_inc(ring_free, RING)
            pe.wait_ge(onehot_ready, 3 * NT)
            zero(aggs[0], True)
            pe.reg_mov(turn, 0)

            def add_rows(layer, g, i, out_sum):
                before = layer * (GROUPS - (i >= LAST))
                pe.wait_ge(slot_full[i], (g + before + 1) * 16)
                for part in range(3):
                    last = mm(out_sum, onehot[:, bass.ds(g * RING + i, 1), :].rearrange("p a n -> p (a n)"),
                              ring[:, i, part * D:(part + 1) * D], start=False, stop=True, skip_group_check=True)
                last.then_inc(ring_free, 1)

            def next_tile(layer, out_sum):
                def turn_over():
                    zero(out_sum, False).then_inc(agg_done, 1)
                    pe.reg_alu(turn, turn, 512, ALU.bitwise_xor)
                    pe.wait_ge(agg_free, node_tile(tile) + layer * NT + 1)
                    zero(sum_at(), True)

                with pe.If(pe.snap(tile) > 0):
                    transposes(node_tile(behind) + (1 + layer) * NT, 0)
                    turn_over()
                    if layer:
                        with pe.If(pe.snap(behind) > 0):
                            slices(node_tile(sliced))
                            pe.reg_add(sliced, sliced, 1)
                        logits(node_tile(behind))
                    else:
                        pe.wait_ge(ld_w2, 16 * (K2 + 1))
                        products(node_tile(behind) + NT, 0, range(CH))
                    pe.reg_add(behind, behind, 1)
                with pe.Else():
                    turn_over()
                pe.reg_add(tile, tile, 1)
                pe.reg_mov(end, pe.value_load(ends[0:1, bass.ds(pe.snap(tile, min_val=0, max_val=NT), 1)]))

            def add_ring(layer, g, n):
                for first in range(0, n, QUAD):
                    slots = range(first, first + QUAD)
                    with pe.If(pe.snap(end) > g * RING + slots[-1]):
                        out_sum = sum_at()
                        for i in slots:
                            add_rows(layer, g, i, out_sum)
                    with pe.Else():
                        for i in slots:
                            out_sum, end_here = sum_at(), pe.snap(end)
                            add_rows(layer, g, i, out_sum)
                            with pe.If(end_here == g * RING + i):
                                next_tile(layer, out_sum)

            for layer in range(2):
                for reg in (tile, behind, sliced):
                    pe.reg_mov(reg, 0)
                pe.reg_mov(end, pe.value_load(ends[0:1, 0:1]))
                if layer:
                    pe.wait_ge(self_free, 2 * NT + 1)
                    for m in range(K2):
                        mm(bank[f"t{m}"][:, :], zeros[:, 0:P], onehot[:, 0:4, :].rearrange("p s n -> p (s n)"),
                           start=True, stop=True, skip_group_check=True)
                with pe.Fori(0, GROUPS - 1) as g:
                    add_ring(layer, g, RING)
                add_ring(layer, GROUPS - 1, LAST)
                if layer:
                    transposes(3 * NT - 1, 0)
                    pe.wait_ge(logit_ready, NT - 1)
                    logits(NT - 1)
                    slices(NT - 2)
                    pe.wait_ge(prev_ready, NT)
                    slices(NT - 1)
                else:
                    transposes(2 * NT - 1, 0)
                    products(2 * NT - 1, 0, range(CH))

            zero(bank["t1"][:, 0:D], False).then_inc(sums_done, 1)
            pe.wait_ge(swsum_steps, NT)
            mm(bank["self"][:, :], ones[:, :], swsum[:, :], start=True, stop=True).then_inc(norm_mm, 1)
            pe.wait_ge(ld_tail, 16 * 2)
            pe.wait_ge(ttn_ready, K2)
            for a in range(HP):
                pair = slice(a * P, (a + 1) * P)
                for k in range(K2):
                    last = mm(bank["c0"][:, pair], wfx[:, k, pair], ttn[:, k, pair], start=(k == 0), stop=(k == K2 - 1))
            last.then_inc(tok_mm, 1)
            pe.wait_ge(tok_ready, 1)
            tok = tokC.rearrange("p a g -> p (a g)")
            for name, to in (("q", "agg0"), ("k", "tr"), ("v", "self")):
                last = mm(bank[to][:, 0:HP * G], bd[name][:, :], tok, start=True, stop=True)
            last.then_inc(qkv_mm, 1)
            pe.wait_ge(qkv_saved, 3)
            qT, kT, vT = qkvT
            for h2 in range(2):
                rows = slice(h2 * G, (h2 + 1) * G)
                for a in range(HP):
                    last = mm(bank[f"t{h2}"][rows, a * G:(a + 1) * G], qT[rows, a, :], kT[rows, a, :], start=True, stop=True)
            last.then_inc(score_mm, 1)
            for h2 in range(2):
                rows = slice(h2 * G, (h2 + 1) * G)
                for a in range(HP):
                    last = mm(bank[VO_BANKS[2 * h2 + a // 2]][0:G, (a % 2) * D:(a % 2 + 1) * D], vT[rows, a, :], wout[rows, a, :], start=True, stop=True)
            last.then_inc(vo_mm, 1)
            pe.wait_ge(att_ready, 1)
            for a in range(HP):
                last = nc.tensor.transpose(bank["agg1"][0:G, a * P:(a + 1) * P], att[:, a, :], ident[:, :])
            last.then_inc(attT_mm, 1)
            pe.wait_ge(attT_saved, 1)
            pe.wait_ge(vo_saved, 4)
            for h2 in range(2):
                rows = slice(h2 * G, (h2 + 1) * G)
                for a in range(HP):
                    last = mm(bank[MIX_BANKS[a // 2]][rows, (a % 2) * D:(a % 2 + 1) * D], attT[0:G, a, rows], vo[0:G, 2 * a + h2, :], start=True, stop=True)
            last.then_inc(mix_mm, 1)
            pe.wait_ge(mix_saved, 2)
            pe.sem_inc(out_mm, 2)
            with pe.Fori(0, NT // 2) as jj:
                for par in range(2):
                    j = jj * 2 + par
                    pe.wait_ge(tile_copied, j + 1)
                    pe.wait_ge(out_added, j + 1)
                    for a in range(HP):
                        last = mm(bank[f"c{par}"][:, 0:D], swTile[:, par, a, :], mix[:, a, :], start=(a == 0), stop=(a == HP - 1))
                    last.then_inc(out_mm, 1)


_INS = ['x', 'src', 'dst', 'edge_type_8', 'L0_gnn_W1', 'L0_gnn_self_w1', 'L0_gnn_b1', 'L0_gnn_W2', 'L0_gnn_self_w2', 'L0_gnn_b2',
        'L0_ffn_W_fx', 'L0_ffn_b_fx', 'L0_ffn_W_x', 'L0_ffn_b_x', 'L0_ffn_W_slice', 'L0_ffn_b_slice', 'L0_ffn_W_q', 'L0_ffn_W_k',
        'L0_ffn_W_v', 'L0_ffn_W_out', 'L0_ffn_b_out', 'L0_ffn_temperature']


def kernel(**inputs):
    import concourse.bacc as bacc
    from concourse.bass_utils import run_bass_kernel_spmd

    nc = bacc.Bacc("TRN2", target_bir_lowering=False, num_devices=1)
    arrays, args = {}, []
    for name in _INS:
        a = np.ascontiguousarray(inputs[name])
        arrays[f"in_{name}"] = a
        args.append(nc.dram_tensor(f"in_{name}", a.shape, mybir.dt.from_np(a.dtype), kind="ExternalInput").ap())
    out = nc.dram_tensor("out", (N, D), f32, kind="ExternalOutput").ap()
    rgcn_slice_attention(nc, *args, out)
    r = run_bass_kernel_spmd(nc, [arrays], core_ids=[0])
    return r.results[0]["out"]
```
